# Optimizing a Trainium2 kernel written in Bass

```python
import numpy as np
import jax
import jax.numpy as jnp

def _softmax(x, axis=-1):
    return jax.nn.softmax(x, axis=axis)

def _gelu(x):
    return jax.nn.gelu(x, approximate=True)

def _silu(x):
    return jax.nn.silu(x)

def _sigmoid(x):
    return jax.nn.sigmoid(x)

def _layernorm(x, axis=-1, eps=1e-05):
    m = jnp.mean(x, axis=axis, keepdims=True)
    v = jnp.var(x, axis=axis, keepdims=True)
    return (x - m) / jnp.sqrt(v + eps)

def _scatter_add(tgt, idx, src, axis=0):
    return tgt.at[idx].add(src)

def _segment_sum(src, seg, n):
    return jax.ops.segment_sum(src, seg, n)
kernel_name = 'mk_adj_ffn_d1_adj_r2_bdda69'

def setup_inputs(seed: int=0):
    np.random.seed(seed)
    _w = jnp.asarray

    def _rec_inputs():
        import jax
        import jax.numpy as jnp
        _gk = jax.random.key(seed)
        x = -0.000929 + 1 * jax.random.normal(jax.random.fold_in(_gk, 1), (8192, 128), jnp.float32)
        _w = (1.0 + jnp.arange(8192, dtype=jnp.float32)) ** (-0.5)
        _w = _w / _w.mean()
        _pij = jnp.clip(0.000488281 * _w[:, None] * _w[None, :], 0.0, 1.0)
        _a = jax.random.uniform(jax.random.fold_in(_gk, 2), (8192, 8192)) < _pij
        _a = jnp.logical_or(_a, jnp.eye(8192, dtype=bool))
        _af = _a.astype(jnp.float32)
        _af = _af / jnp.maximum(_af.sum(-1, keepdims=True), 1.0)
        adj = _af
        return (x, adj)
    x, adj = _rec_inputs()

    def _L0_gnn_setup():
        import jax, jax.numpy as jnp
        import numpy as np
        from jax import lax
        D_MODEL = 128
        D_STATE = 16
        D_CONV = 4
        EXPAND = 2
        D_INNER = EXPAND * D_MODEL
        DT_RANK = (D_MODEL + 15) // 16
        N = 2048
        EPS = 1e-05

        def _mamba(h, w_in, conv_w, conv_b, w_xp, w_dt, b_dt, A_log, D_skip, w_out):
            L = h.shape[0]
            xz = h @ w_in
            xc, z = (xz[:, :D_INNER], xz[:, D_INNER:])
            xpad = jnp.pad(xc, ((D_CONV - 1, 0), (0, 0)))
            xconv = sum((xpad[k:k + L] * conv_w[:, k] for k in range(D_CONV))) + conv_b
            u = jax.nn.silu(xconv)
            dbc = u @ w_xp
            dt = jax.nn.softplus(dbc[:, :DT_RANK] @ w_dt + b_dt)
            B = dbc[:, DT_RANK:DT_RANK + D_STATE]
            C = dbc[:, DT_RANK + D_STATE:]
            A = -jnp.exp(A_log)
            dA = jnp.exp(dt[:, :, None] * A[None])
            dBu = dt[:, :, None] * B[:, None, :] * u[:, :, None]

            def step(hst, inp):
                dAt, dBut, Ct = inp
                hst = dAt * hst + dBut
                return (hst, hst @ Ct)
            _, ys = lax.scan(step, jnp.zeros((D_INNER, D_STATE), h.dtype), (dA, dBu, C))
            y = ys + u * D_skip
            y = y * jax.nn.silu(z)
            return y @ w_out
        key = jax.random.key(seed)
        ks = jax.random.split(key, 16)
        x = jax.random.normal(ks[0], (N, D_MODEL), dtype=jnp.float32)
        a = jax.random.uniform(ks[1], (N, N), dtype=jnp.float32)
        adj = a / a.sum(axis=1, keepdims=True)
        s = lambda fi, fo: 1.0 / np.sqrt(fi)
        gcn_w = jax.random.uniform(ks[2], (D_MODEL, D_MODEL), jnp.float32, -s(D_MODEL, 0), s(D_MODEL, 0))
        gcn_b = jnp.zeros((D_MODEL,), jnp.float32)
        ln_g = jnp.ones((D_MODEL,), jnp.float32)
        ln_b = jnp.zeros((D_MODEL,), jnp.float32)
        w_in = jax.random.normal(ks[3], (D_MODEL, 2 * D_INNER), jnp.float32) * s(D_MODEL, 0)
        conv_w = jax.random.normal(ks[4], (D_INNER, D_CONV), jnp.float32) * s(D_CONV, 0)
        conv_b = jnp.zeros((D_INNER,), jnp.float32)
        w_xp = jax.random.normal(ks[5], (D_INNER, DT_RANK + 2 * D_STATE), jnp.float32) * s(D_INNER, 0)
        w_dt = jax.random.normal(ks[6], (DT_RANK, D_INNER), jnp.float32) * s(DT_RANK, 0)
        b_dt = jnp.log(jnp.expm1(jnp.exp(jax.random.uniform(ks[7], (D_INNER,), jnp.float32, np.log(0.001), np.log(0.1)))))
        A_log = jnp.log(jnp.broadcast_to(jnp.arange(1, D_STATE + 1, dtype=jnp.float32), (D_INNER, D_STATE)))
        D_skip = jnp.ones((D_INNER,), jnp.float32)
        w_out = jax.random.normal(ks[8], (D_INNER, D_MODEL), jnp.float32) * s(D_INNER, 0)
        return dict(x=x, adj=adj, gcn_w=gcn_w, gcn_b=gcn_b, ln_g=ln_g, ln_b=ln_b, w_in=w_in, conv_w=conv_w, conv_b=conv_b, w_xp=w_xp, w_dt=w_dt, b_dt=b_dt, A_log=A_log, D_skip=D_skip, w_out=w_out)
    _L0_gnn_all = _L0_gnn_setup()
    _L0_gnn_in = {k: v for k, v in _L0_gnn_all.items() if k in ('gcn_w', 'gcn_b', 'ln_g', 'ln_b', 'w_in', 'conv_w', 'conv_b', 'w_xp', 'w_dt', 'b_dt', 'A_log', 'D_skip', 'w_out')}
    del _L0_gnn_all

    def _L0_ffn_setup():
        import jax, jax.numpy as jnp
        import numpy as np
        B, T, D, H, L = (16, 2048, 128, 128, 2)

        def _lstm(x, W_ih, W_hh, b_ih, b_hh):
            x_proj = jnp.einsum('btd,gd->btg', x, W_ih) + b_ih + b_hh
            h0 = jnp.zeros((x.shape[0], W_hh.shape[1]), x.dtype)
            c0 = jnp.zeros_like(h0)

            def step(carry, xp):
                h, c = carry
                gates = xp + h @ W_hh.T
                i, f, g, o = jnp.split(gates, 4, axis=-1)
                c = jax.nn.sigmoid(f) * c + jax.nn.sigmoid(i) * jnp.tanh(g)
                h = jax.nn.sigmoid(o) * jnp.tanh(c)
                return ((h, c), h)
            _, hs = jax.lax.scan(step, (h0, c0), jnp.swapaxes(x_proj, 0, 1))
            return jnp.swapaxes(hs, 0, 1)
        key = jax.random.key(seed)
        ks = jax.random.split(key, 9)
        s = 1.0 / np.sqrt(H)
        u = lambda k, shape: jax.random.uniform(k, shape, jnp.float32, -s, s)
        return {'x': jax.random.normal(ks[0], (B, T, D), jnp.float32), 'W_ih': u(ks[1], (4 * H, D)), 'W_hh': u(ks[2], (4 * H, H)), 'b_ih': u(ks[3], (4 * H,)), 'b_hh': u(ks[4], (4 * H,)), 'W_lin': u(ks[5], (L, H)), 'b_lin': u(ks[6], (L,)), 'fw_att': jnp.full((1, H), 0.001, jnp.float32), 'bw_att': jnp.full((1, H), 0.001, jnp.float32)}
    _L0_ffn_all = _L0_ffn_setup()
    _L0_ffn_in = {k: v for k, v in _L0_ffn_all.items() if k in ('W_ih', 'W_hh', 'b_ih', 'b_hh', 'W_lin', 'b_lin', 'fw_att', 'bw_att')}
    del _L0_ffn_all
    return {'x': x, 'adj': adj, 'L0_gnn_gcn_w': _L0_gnn_in['gcn_w'], 'L0_gnn_gcn_b': _L0_gnn_in['gcn_b'], 'L0_gnn_ln_g': _L0_gnn_in['ln_g'], 'L0_gnn_ln_b': _L0_gnn_in['ln_b'], 'L0_gnn_w_in': _L0_gnn_in['w_in'], 'L0_gnn_conv_w': _L0_gnn_in['conv_w'], 'L0_gnn_conv_b': _L0_gnn_in['conv_b'], 'L0_gnn_w_xp': _L0_gnn_in['w_xp'], 'L0_gnn_w_dt': _L0_gnn_in['w_dt'], 'L0_gnn_b_dt': _L0_gnn_in['b_dt'], 'L0_gnn_A_log': _L0_gnn_in['A_log'], 'L0_gnn_D_skip': _L0_gnn_in['D_skip'], 'L0_gnn_w_out': _L0_gnn_in['w_out'], 'L0_ffn_W_ih': _L0_ffn_in['W_ih'], 'L0_ffn_W_hh': _L0_ffn_in['W_hh'], 'L0_ffn_b_ih': _L0_ffn_in['b_ih'], 'L0_ffn_b_hh': _L0_ffn_in['b_hh'], 'L0_ffn_W_lin': _L0_ffn_in['W_lin'], 'L0_ffn_b_lin': _L0_ffn_in['b_lin'], 'L0_ffn_fw_att': _L0_ffn_in['fw_att'], 'L0_ffn_bw_att': _L0_ffn_in['bw_att']}

def reference(x, adj, L0_gnn_gcn_w, L0_gnn_gcn_b, L0_gnn_ln_g, L0_gnn_ln_b, L0_gnn_w_in, L0_gnn_conv_w, L0_gnn_conv_b, L0_gnn_w_xp, L0_gnn_w_dt, L0_gnn_b_dt, L0_gnn_A_log, L0_gnn_D_skip, L0_gnn_w_out, L0_ffn_W_ih, L0_ffn_W_hh, L0_ffn_b_ih, L0_ffn_b_hh, L0_ffn_W_lin, L0_ffn_b_lin, L0_ffn_fw_att, L0_ffn_bw_att):
    import jax
    import jax.numpy as jnp

    def _L0_gnn_ref(x, adj, gcn_w, gcn_b, ln_g, ln_b, w_in, conv_w, conv_b, w_xp, w_dt, b_dt, A_log, D_skip, w_out):
        import jax, jax.numpy as jnp
        import numpy as np
        from jax import lax
        D_MODEL = 128
        D_STATE = 16
        D_CONV = 4
        EXPAND = 2
        D_INNER = EXPAND * D_MODEL
        DT_RANK = (D_MODEL + 15) // 16
        N = 2048
        EPS = 1e-05

        def _mamba(h, w_in, conv_w, conv_b, w_xp, w_dt, b_dt, A_log, D_skip, w_out):
            L = h.shape[0]
            xz = h @ w_in
            xc, z = (xz[:, :D_INNER], xz[:, D_INNER:])
            xpad = jnp.pad(xc, ((D_CONV - 1, 0), (0, 0)))
            xconv = sum((xpad[k:k + L] * conv_w[:, k] for k in range(D_CONV))) + conv_b
            u = jax.nn.silu(xconv)
            dbc = u @ w_xp
            dt = jax.nn.softplus(dbc[:, :DT_RANK] @ w_dt + b_dt)
            B = dbc[:, DT_RANK:DT_RANK + D_STATE]
            C = dbc[:, DT_RANK + D_STATE:]
            A = -jnp.exp(A_log)
            dA = jnp.exp(dt[:, :, None] * A[None])
            dBu = dt[:, :, None] * B[:, None, :] * u[:, :, None]

            def step(hst, inp):
                dAt, dBut, Ct = inp
                hst = dAt * hst + dBut
                return (hst, hst @ Ct)
            _, ys = lax.scan(step, jnp.zeros((D_INNER, D_STATE), h.dtype), (dA, dBu, C))
            y = ys + u * D_skip
            y = y * jax.nn.silu(z)
            return y @ w_out
        h = jax.nn.relu(adj @ x @ gcn_w + gcn_b)
        mu = h.mean(-1, keepdims=True)
        var = h.var(-1, keepdims=True)
        h = (h - mu) * lax.rsqrt(var + EPS) * ln_g + ln_b
        return _mamba(h, w_in, conv_w, conv_b, w_xp, w_dt, b_dt, A_log, D_skip, w_out)

    def _L0_ffn_ref(x, W_ih, W_hh, b_ih, b_hh, W_lin, b_lin, fw_att, bw_att):
        import jax, jax.numpy as jnp
        import numpy as np
        B, T, D, H, L = (16, 2048, 128, 128, 2)

        def _lstm(x, W_ih, W_hh, b_ih, b_hh):
            x_proj = jnp.einsum('btd,gd->btg', x, W_ih) + b_ih + b_hh
            h0 = jnp.zeros((x.shape[0], W_hh.shape[1]), x.dtype)
            c0 = jnp.zeros_like(h0)

            def step(carry, xp):
                h, c = carry
                gates = xp + h @ W_hh.T
                i, f, g, o = jnp.split(gates, 4, axis=-1)
                c = jax.nn.sigmoid(f) * c + jax.nn.sigmoid(i) * jnp.tanh(g)
                h = jax.nn.sigmoid(o) * jnp.tanh(c)
                return ((h, c), h)
            _, hs = jax.lax.scan(step, (h0, c0), jnp.swapaxes(x_proj, 0, 1))
            return jnp.swapaxes(hs, 0, 1)
        lstm_out = _lstm(x, W_ih, W_hh, b_ih, b_hh)
        logits = jnp.einsum('bth,lh->btl', lstm_out, W_lin) + b_lin
        g = jax.lax.stop_gradient(jnp.argmax(logits, axis=-1).astype(lstm_out.dtype))[..., None]
        w = g * lstm_out
        inc = jnp.cumsum(w, axis=1)
        prefix = inc - w
        suffix = inc[:, -1:, :] - inc
        return 2.0 * lstm_out + prefix * fw_att + suffix * bw_att
    x = x + _L0_gnn_ref(_layernorm(x, axis=-1), adj, L0_gnn_gcn_w, L0_gnn_gcn_b, L0_gnn_ln_g, L0_gnn_ln_b, L0_gnn_w_in, L0_gnn_conv_w, L0_gnn_conv_b, L0_gnn_w_xp, L0_gnn_w_dt, L0_gnn_b_dt, L0_gnn_A_log, L0_gnn_D_skip, L0_gnn_w_out)
    x = x + _L0_ffn_ref(_layernorm(x, axis=-1)[None], L0_ffn_W_ih, L0_ffn_W_hh, L0_ffn_b_ih, L0_ffn_b_hh, L0_ffn_W_lin, L0_ffn_b_lin, L0_ffn_fw_att, L0_ffn_bw_att)[0]
    return x

_drawn_inputs = setup_inputs


def setup_inputs(seed=0):
    import zlib

    import numpy as np

    out = dict(_drawn_inputs(seed))
    spreads = {'L0_gnn_gcn_b': (0.0, 0.1),
     'L0_gnn_ln_g': (1.0, 0.2),
     'L0_gnn_ln_b': (0.0, 0.1),
     'L0_gnn_conv_b': (0.0, 0.1),
     'L0_gnn_D_skip': (1.0, 0.2),
     'L0_ffn_fw_att': (0.0010000000474974513, 0.2),
     'L0_ffn_bw_att': (0.0010000000474974513, 0.2)}
    factors = {}
    for name, (base, spread) in spreads.items():
        noise = np.random.default_rng([zlib.crc32(name.encode()), seed]).standard_normal(out[name].shape)
        drawn = base * np.exp(spread * noise) if base else spread * noise
        out[name] = jnp.asarray(drawn.astype(out[name].dtype))
    for name, factor in factors.items():
        out[name] = (out[name] * factor).astype(out[name].dtype)
    return out
```

```python
from contextlib import ExitStack

import numpy as np

import concourse.bass as bass
from concourse import mybir

N = 8192
D = 128
P = 128
CH = 512
NC = N // CH
BLK = N // P
PB = 4
PIECES = BLK // PB
RING = 4
DI = 256
HV = DI // P
DS = 16
TAPS = 4
HALO = TAPS - 1
DR = 8
BC = 2 * DS
XPW = 3 * BC + DR
SEG = 32
NSEG = N // SEG
SPC = CH // SEG
HS = NSEG // 2
EPS = 1e-5
TOL = 2.0 ** -21
PARTS = 3

WSIZE = dict(gcn=D, w_in=2 * DI, w_xp=HV * XPW, w_dt=DI, w_out=HV * D, w_ih=4 * D, w_hh=4 * D)
WOFF, _o = {}, 0
for _n, _s in WSIZE.items():
    WOFF[_n] = _o
    _o += _s
WTOT = _o
VSIZE = dict(gcn_b=1, ln_g=1, ln_b=1, conv_b=HV, conv_w=HV * TAPS, b_dt=HV, d_skip=HV, fw=1, bw=1,
             a_log=HV * DS, w_lin=2, b_lin=2)
VOFF, _o = {}, 0
for _n, _s in VSIZE.items():
    VOFF[_n] = _o
    _o += _s
VTOT = _o

SHARED = [("gcn", 0, "pre"), ("mean", 2, "pre"), ("out", 3, "post"), ("var", 4, "pre"),
          ("pmean", 5, "post"), ("xc0", 6, "pre"), ("xc1", 6, "pre"), ("z0", 7, "pre"),
          ("z1", 7, "pre"), ("pvar", 8, "post"), ("dbc", 10, "pre"), ("dt0", 12, "pre"),
          ("dt1", 12, "pre")]
PRE_STEPS = sum(s[2] == "pre" for s in SHARED)
POST_STEPS = sum(s[2] == "post" for s in SHARED)


def shared_index(step, k, pre, post):
    if isinstance(k, int):
        before = PRE_STEPS * (min(k, NC + 1) - 1) + POST_STEPS * max(0, k - 3)
    else:
        before = (PRE_STEPS + POST_STEPS) * k - (PRE_STEPS + 3 * POST_STEPS)
    names = [s[0] for s in SHARED if (pre and s[2] == "pre") or (post and s[2] == "post")]
    return before + names.index(step)


def wait(eng, sem, value):
    if not (isinstance(value, int) and value <= 0):
        eng.wait_ge(sem, value)


def build(nc, adj_t, x_rows, x_t, weights, vectors, lstm_bias, out_t):
    F32, BF, I32 = mybir.dt.float32, mybir.dt.bfloat16, mybir.dt.int32
    ALU, ACT, AX = mybir.AluOpType, mybir.ActivationFunctionType, mybir.AxisListType

    x1_dram = nc.dram_tensor("x1_scratch", (NC, P, CH), F32, kind="Internal").ap()
    xl_dram = nc.dram_tensor("xl_scratch", (NC, P, CH), F32, kind="Internal").ap()

    ctx = ExitStack()
    with ctx:
        def sb(name, shape, dt=F32):
            return ctx.enter_context(nc.sbuf_tensor(name, shape, dt))

        def sem(name):
            return ctx.enter_context(nc.semaphore(name))

        xh = sb("xh", [P, (SEG + 1) * NSEG])
        xn = xh[:, 0:N].rearrange("p (b d) -> p b d", d=D)
        hs = xh[:, :].rearrange("p (t s) -> p t s", s=NSEG)
        ring = sb("ring", [P, RING * PB * CH])
        xls = ring[:, :].rearrange("p (c t) -> p c t", c=NC)
        w_sb = sb("w_sb", [P, WTOT])
        v_sb = sb("v_sb", [P, VTOT])
        sel = sb("sel", [PARTS * BC, BC * P], BF)
        mean_w = sb("mean_w", [P, P])
        ones_w = sb("ones_w", [P, P])
        eps = sb("eps", [P, 1])
        minus1 = sb("minus1", [P, 1])
        a_neg = sb("a_neg", [P, HV * DS])
        negbw = sb("negbw", [P, 1])
        bc_parts = [sb(f"bc_parts{i}", [PARTS * BC, CH], BF) for i in range(2)]
        bc_mid = sb("bc_mid", [PARTS * BC, CH], BF)
        hstate = sb("hstate", [P, DS * HV])
        bias_in = sb("bias_in", [PARTS * BC, 2 * P])
        bias_mid = sb("bias_mid", [PARTS * BC, P], BF)
        bias_w = sb("bias_w", [PARTS * BC, P], BF)
        flag = sb("flag", [1, 1], I32)
        table_pad = sb("table_pad", [P, 1])
        run_total = sb("run_total", [P, 1])[:, :]

        WORK = 29 * 1024 + 512
        work = sb("work", [P, WORK])
        at = [0]

        def carve(n):
            a = at[0]
            at[0] += n
            assert at[0] <= WORK, at[0]
            return work[:, a:a + n]

        def halves(ap):
            return ap.rearrange("p (h t) -> p h t", h=HV)

        W2 = HV * CH
        dbu = [halves(carve(W2)) for _ in range(2)]
        hb = [halves(carve(W2)) for _ in range(2)]
        hc = [halves(carve(W2)) for _ in range(2)]
        xc = [halves(carve(HV * (HALO + CH + 1))) for _ in range(2)]
        u = [halves(carve(W2)) for _ in range(2)]
        sz = [halves(carve(W2)) for _ in range(2)]
        dt = [halves(carve(W2)) for _ in range(2)]
        dtu = [halves(carve(W2)) for _ in range(2)]
        acc = halves(carve(W2))
        yv = halves(carve(W2))
        wa, wb, wc, wd = (halves(carve(W2)) for _ in range(4))
        taps = [wd, wa, wb, wc]
        m1, ht, sq, rs = (carve(CH) for _ in range(4))
        dbc, r1 = carve(CH), carve(CH)
        xt = [carve(CH) for _ in range(2)]
        x1c, xd, psq, prs = (carve(CH) for _ in range(4))
        xlc = carve(CH)
        sq_rows = work[:, 0:16 * D].rearrange("p (b d) -> p b d", d=D)
        stat = work[:, 4096:4096 + 4 * BLK].rearrange("p (k b) -> p k b", k=4)
        at[0] = 0
        inc_all = carve(N)
        fin_all = carve(N)
        c_in = carve(NSEG)
        c_st = carve(NSEG)
        sg = [carve(3 * HS) for _ in range(2)]
        tg = [carve(HS) for _ in range(2)]
        fc = [carve(HS) for _ in range(2)]
        ig = [carve(HS) for _ in range(2)]
        tc = [carve(HS) for _ in range(2)]
        diff = carve(2 * (NSEG - 1))
        agree = carve(1)
        alive = carve(1)
        passes = carve(1)
        wlin = carve(2 * P)
        l0b = [carve(CH) for _ in range(2)]
        gsel = [carve(CH) for _ in range(2)]
        wsel = [carve(CH) for _ in range(2)]
        x1f = [carve(CH) for _ in range(2)]
        ob = [carve(CH) for _ in range(2)]
        h2 = [carve(CH) for _ in range(2)]

        def W(name, lo=0, hi=None):
            o = WOFF[name]
            return w_sb[:, o + lo:o + (WSIZE[name] if hi is None else hi)]

        def V(name, i=0):
            return v_sb[:, VOFF[name] + i:VOFF[name] + i + 1]

        bank = [ctx.enter_context(nc.psum_tensor(f"bank{i}", [P, CH], F32)) for i in range(8)]
        mixed, shared = bank[0], bank[2]
        da = [bank[1], bank[7]]
        b_bank = [bank[3], bank[4]]
        c_bank = [bank[5], bank[6]]
        gates = [[bank[0], bank[1]], [bank[2], bank[3]]]
        count_ps = bank[4]
        l_bank = [[bank[0], bank[1]], [bank[2], bank[3]]]

        consts_in, x_in, bias_loaded = sem("consts_in"), sem("x_in"), sem("bias_loaded")
        consts_ready, sel_ready, init_done = sem("consts_ready"), sem("sel_ready"), sem("init_done")
        row_sum, row_mean, row_centred, row_sq = sem("row_sum"), sem("row_mean"), sem("row_centred"), sem("row_sq")
        row_var, row_ln, row_rstd, xn_ready = sem("row_var"), sem("row_ln"), sem("row_rstd"), sem("xn_ready")
        adj_in = [sem(f"adj_in{i}") for i in range(RING)]
        adj_used = sem("adj_used")
        mixed_copied = sem("mixed_copied")
        shared_written, shared_read = sem("shared_written"), sem("shared_read")
        squared = sem("squared")
        lnv_ready, rstd_ready, hn_ready, h_ready = sem("lnv_ready"), sem("rstd_ready"), sem("hn_ready"), sem("h_ready")
        xc_ready, tap_ready, tap_done, conv_ready = sem("xc_ready"), sem("tap_ready"), sem("tap_done"), sem("conv_ready")
        halo_ready = sem("halo_ready")
        z_raw, u_ready, sz_ready = sem("z_raw"), sem("u_ready"), sem("sz_ready")
        high_ready, r1_ready = sem("high_ready"), sem("r1_ready")
        mid_rounded, mid_ready, low_ready = sem("mid_rounded"), sem("mid_ready"), sem("low_ready")
        pos_dt, exp_dt, one_dt, log_dt, less_dt = (sem(f"{n}_dt") for n in ("pos", "exp", "one", "log", "less"))
        rem_dt, sum_dt, dt_ready, dtu_ready = sem("rem_dt"), sem("sum_dt"), sem("dt_ready"), sem("dtu_ready")
        b_ready, c_ready, da_ready = sem("b_ready"), sem("c_ready"), sem("da_ready")
        dbu_done, scan_done, hc_done, state_saved = sem("dbu_done"), sem("scan_done"), sem("hc_done"), sem("state_saved")
        y_added, skip_ready, y_skip, y_ready = (sem(n) for n in ("y_added", "skip_ready", "y_skip", "y_ready"))
        xt_in, x1_stored = [sem(f"xt_in{i}") for i in range(2)], sem("x1_stored")
        psq_ready, plnv_ready, prstd_ready = sem("psq_ready"), sem("plnv_ready"), sem("prstd_ready")
        xl_ready, xl_stored = sem("xl_ready"), sem("xl_stored")
        xls_in, lstm_init = sem("xls_in"), sem("lstm_init")
        bias_ready = sem("bias_ready")
        gates_ready = sem("gates_ready")
        tg_ready, sg_ready, fc_ready, ig_ready = sem("tg_ready"), sem("sg_ready"), sem("fc_ready"), sem("ig_ready")
        cell_ready, tc_ready, hid_ready = sem("cell_ready"), sem("tc_ready"), sem("hid_ready")
        flag_seen = sem("flag_seen")
        agree_ready, agree_sum, flag_ready, check_step = sem("agree_ready"), sem("agree_sum"), sem("flag_ready"), sem("check_step")
        l0_ready, l1_ready, l0b_ready, gsel_ready = sem("l0_ready"), sem("l1_ready"), sem("l0b_ready"), sem("gsel_ready")
        wsel_ready, inc_ready, dbl_ready, h2_ready = sem("wsel_ready"), sem("inc_ready"), sem("dbl_ready"), sem("h2_ready")
        x1f_in, out_done = ([sem(f"{n}{i}") for i in range(2)] for n in ("x1f_in", "out_done"))
        fwd_done, pre_ready, suf_ready, ob_ready = (sem(n) for n in ("fwd_done", "pre_ready", "suf_ready", "ob_ready"))

        block = ctx.enter_context(nc.Block())

        def iterations(eng, step):
            def flags(k):
                return k < NC, 1 <= k <= NC, 2 <= k <= NC + 1, 3 <= k <= NC + 2
            for k in range(4):
                step(k, k % 2, *flags(k))
            with eng.Fori(4, NC - 1, 2) as k:
                step(k, 0, True, True, True, True)
                step(k + 1, 1, True, True, True, True)
            for k in range(NC, NC + 3):
                step(k, k % 2, *flags(k))

        def by_chunk(eng, step):
            for c in range(2):
                step(c, c)
            with eng.Fori(2, NC - 1, 2) as c:
                step(c, 0)
                step(c + 1, 1)

        @block.sync
        def _(sp):
            sp.dma_start(xh[:, 0:N], x_rows).then_inc(x_in, 16)
            sp.dma_start(w_sb[:, :], weights).then_inc(consts_in, 16)
            sp.dma_start(v_sb[:, :], vectors).then_inc(consts_in, 16)

            def step(k, par, adj, pre, scan, post):
                if post:
                    wait(sp, x1_stored, 16 * (k - 4))
                    sp.dma_start(xt[1 - par], x_t[k - 3]).then_inc(xt_in[1 - par], 16)
                if adj:
                    for j in range(PIECES):
                        r = j % RING
                        wait(sp, adj_used, PIECES * k + (j - RING + 1))
                        sp.dma_start(ring[:, r * PB * CH:(r + 1) * PB * CH],
                                     adj_t[k, :, j * PB * CH:(j + 1) * PB * CH]).then_inc(adj_in[r], 16)

            iterations(sp, step)
            sp.wait_ge(adj_used, PIECES * NC)
            sp.wait_ge(xl_stored, 16 * NC)
            sp.dma_start(xls, xl_dram.rearrange("c p t -> p c t")).then_inc(xls_in, 16)
            sp.wait_ge(x1_stored, 16 * NC)
            sp.wait_ge(prstd_ready, NC)
            def chunk(i, q):
                wait(sp, dbl_ready, i - 1)
                sp.dma_start(x1f[q], x1_dram[i]).then_inc(x1f_in[q], 16)

            by_chunk(sp, chunk)
            def chunk(i, q):
                sp.wait_ge(ob_ready, i + 1)
                sp.dma_start(out_t[i], ob[q]).then_inc(out_done[q], 16)

            by_chunk(sp, chunk)
            for q in range(2):
                sp.wait_ge(out_done[q], 8 * NC)

        @block.tensor
        def _(pe):
            pe.wait_ge(consts_in, 32)
            pe.wait_ge(consts_ready, 1)
            pe.wait_ge(sel_ready, 4)

            def step(k, par, adj, pre, scan, post):
                cs = k - 2

                def shared_step(name):
                    i = shared_index(name, k, pre, post)
                    wait(pe, shared_read, i)
                    out = shared[:, :]
                    if name == "gcn":
                        pe.wait_ge(mixed_copied, k)
                        ins = [(W("gcn"), m1)]
                    elif name == "mean":
                        ins = [(mean_w[:, :], ht)]
                    elif name == "var":
                        pe.wait_ge(squared, k)
                        ins = [(mean_w[:, :], sq)]
                    elif name in ("xc0", "xc1", "z0", "z1"):
                        b = ("xc0", "xc1", "z0", "z1").index(name)
                        pe.wait_ge(h_ready, k)
                        ins = [(W("w_in", b * P, (b + 1) * P), ht)]
                    elif name == "dbc":
                        pe.wait_ge(u_ready, k)
                        out = shared[0:XPW, :]
                        ins = [(W("w_xp", h * XPW, (h + 1) * XPW), u[1 - par][:, h, :]) for h in range(HV)]
                    elif name in ("dt0", "dt1"):
                        h = int(name[2])
                        o = WOFF["w_dt"] + h * P
                        ins = [(w_sb[0:XPW, o:o + P], dbc[0:XPW, :])]
                    elif name == "out":
                        pe.wait_ge(y_ready, k - 2)
                        ins = [(W("w_out", h * D, (h + 1) * D), yv[:, h, :]) for h in range(HV)]
                    elif name == "pmean":
                        ins = [(mean_w[:, :], x1c)]
                    else:
                        pe.wait_ge(psq_ready, k - 2)
                        ins = [(mean_w[:, :], psq)]
                    for n, (a, b) in enumerate(ins):
                        last = nc.tensor.matmul(out, a, b, start=(n == 0), stop=(n == len(ins) - 1))
                    last.then_inc(shared_written, 1)

                def spread(bank_, used, ready, row, n):
                    wait(pe, used, DS * cs + (n - 1))
                    nc.tensor.matmul(bank_[n % 2][:, :], sel[:, row * P:(row + 1) * P],
                                     bc_parts[par][:, :], start=True, stop=True).then_inc(ready, 1)

                for s in range(16):
                    if scan:
                        if s == 0:
                            pe.wait_ge(low_ready, cs + 1)
                            pe.wait_ge(mid_ready, cs + 1)
                            spread(b_bank, dbu_done, b_ready, 0, 0)
                        if s >= 1:
                            spread(c_bank, hc_done, c_ready, DS + s - 1, s - 1)
                        if s < DS - 1:
                            spread(b_bank, dbu_done, b_ready, s + 1, s + 1)
                    for name, slot, stage in SHARED:
                        if slot == s and ((stage == "pre" and pre) or (stage == "post" and post)):
                            shared_step(name)
                    if adj:
                        if s == 0:
                            wait(pe, mixed_copied, k)
                        r = s % RING
                        if not scan:
                            if isinstance(k, int) and k == 0 and s % 4 == 0:
                                pe.wait_ge(xn_ready, s // 4 + 1)
                        pe.wait_ge(adj_in[r], 16 * (PIECES // RING) * k + 16 * (s // RING + 1))
                        for b in range(PB):
                            j = s * PB + b
                            a = ring[:, (r * PB + b) * CH:(r * PB + b + 1) * CH]
                            last = nc.tensor.matmul(mixed[:, :], xn[:, j, :], a, start=(j == 0), stop=(j == BLK - 1))
                        last.then_inc(adj_used, 1)
                if scan:
                    spread(c_bank, hc_done, c_ready, 2 * DS - 1, DS - 1)

            iterations(pe, step)

            pe.wait_ge(xls_in, 16)
            pe.wait_ge(bias_ready, 1)
            pe.wait_ge(lstm_init, 2)
            pass_no = pe.alloc_register("pe_pass")
            go_on = pe.alloc_register("pe_go")
            pe.reg_mov(pass_no, 0)
            pe.reg_mov(go_on, 1)

            def input_part(t, tau_par, b):
                g = gates[b][tau_par]
                nc.tensor.matmul(g[:, :], bias_w[:, :], sel[:, 0:4 * P], start=True, stop=False, skip_group_check=True)
                for q in (3, 0, 1, 2):
                    nc.tensor.matmul(g[:, q * HS:(q + 1) * HS], W("w_ih", q * D, (q + 1) * D),
                                     xls[:, b * (NC // 2):(b + 1) * (NC // 2), bass.ds(t * SPC, SPC)],
                                     start=False, stop=False, skip_group_check=True)

            def hidden_part(t, tau_par, b, done):
                g = gates[b][tau_par]
                wait(pe, hid_ready, done)
                for q in (3, 0, 1, 2):
                    last = nc.tensor.matmul(g[:, q * HS:(q + 1) * HS], W("w_hh", q * D, (q + 1) * D),
                                            hs[:, t, b * HS:(b + 1) * HS],
                                            start=False, stop=(q == 2), skip_group_check=True)
                last.then_inc(gates_ready, 1)

            with pe.While(lambda: pe.snap(go_on)):
                pn = pe.snap(pass_no)
                for b in range(2):
                    input_part(0, 0, b)

                def two_steps(t, last_pair):
                    for e in range(2):
                        for b in range(2):
                            first = isinstance(t, int) and t + e == 0
                            hidden_part(t + e, e, b, 0 if first else 2 * SEG * pn + 2 * (t + e) + (b - 1))
                            if not (last_pair and e == 1):
                                input_part(t + e + 1, 1 - e, b)

                two_steps(0, False)
                with pe.Fori(2, SEG - 3, 2) as t:
                    two_steps(t, False)
                two_steps(SEG - 2, True)
                pe.wait_ge(agree_ready, pn + 1)
                nc.tensor.matmul(count_ps[:, 0:1], ones_w[:, :], agree, start=True, stop=True).then_inc(agree_sum, 1)
                pe.wait_ge(flag_ready, pn + 1)
                pe.sem_inc(flag_seen, 1)
                pe.reg_load(go_on, flag[0:1, 0:1])
                pe.reg_add(pass_no, pass_no, 1)

            pe.wait_ge(lstm_init, 3)
            def chunk(i, q):
                for l, ready, used in ((0, l0_ready, l0b_ready), (1, l1_ready, gsel_ready)):
                    wait(pe, used, i - 1)
                    nc.tensor.matmul(l_bank[l][q][:, :], wlin[:, l * P:(l + 1) * P],
                                     hs[:, 1:SEG + 1, bass.ds(i * SPC, SPC)],
                                     start=True, stop=True).then_inc(ready, 1)

            by_chunk(pe, chunk)

        @block.scalar
        def _(act):
            act.dma_start(bias_in[0:4, :], lstm_bias).then_inc(bias_loaded, 16)
            act.dma_start(bias_in[32:36, :], lstm_bias).then_inc(bias_loaded, 16)
            act.dma_start(bias_in[64:68, :], lstm_bias).then_inc(bias_loaded, 16)
            act.wait_ge(consts_ready, 1)
            for g in range(4):
                act.wait_ge(row_centred, g + 1)
                if g:
                    act.wait_ge(row_var, g)
                nc.scalar.activation(sq_rows, xn[:, 16 * g:16 * g + 16, :], ACT.Square).then_inc(row_sq, 1)
                act.wait_ge(row_var, g + 1)
                nc.scalar.activation(stat[:, 2, 16 * g:16 * g + 16], stat[:, 1, 16 * g:16 * g + 16], ACT.Ln,
                                     bias=eps[:, :], scale=1.0 / D).then_inc(row_ln, 1)
                act.wait_ge(row_ln, g + 1)
                nc.scalar.activation(stat[:, 3, 16 * g:16 * g + 16], stat[:, 2, 16 * g:16 * g + 16], ACT.Exp,
                                     scale=-0.5).then_inc(row_rstd, 1)
            act.wait_ge(consts_in, 32)
            o = VOFF["a_log"]
            nc.scalar.activation(a_neg[:, :], v_sb[:, o:o + HV * DS], ACT.Exp).then_inc(init_done, 1)

            def step(k, par, adj, pre, scan, post):
                cs, q = k - 2, 1 - par

                def written(name):
                    act.wait_ge(shared_written, shared_index(name, k, pre, post) + 1)

                def pre_part(s):
                    if s == 0:
                        written("gcn")
                        nc.scalar.activation(ht, shared[:, :], ACT.Relu, bias=V("gcn_b")).then_inc(shared_read, 1)
                    if s == 2:
                        act.wait_ge(shared_read, shared_index("mean", k, pre, post) + 1)
                        nc.scalar.activation(sq, ht, ACT.Square).then_inc(squared, 1)
                    if s == 4:
                        written("var")
                        nc.scalar.activation(rs, shared[:, :], ACT.Ln, bias=eps[:, :]).then_inc(shared_read, 1)
                        act.wait_ge(shared_read, shared_index("var", k, pre, post) + 1)
                        nc.scalar.activation(rs, rs, ACT.Exp, scale=-0.5).then_inc(rstd_ready, 1)
                    if s == 5:
                        act.wait_ge(hn_ready, k)
                        nc.scalar.activation(ht, ht, ACT.Identity, bias=V("ln_b"), scale=V("ln_g")).then_inc(h_ready, 1)
                    if s == 6:
                        for h in range(HV):
                            written(f"xc{h}")
                            nc.scalar.activation(xc[q][:, h, HALO:HALO + CH], shared[:, :], ACT.Copy).then_inc(shared_read, 1)
                        act.wait_ge(shared_read, shared_index("xc1", k, pre, post) + 1)
                        act.wait_ge(halo_ready, k)
                        for i, w in enumerate(taps):
                            for h in range(HV):
                                last = nc.scalar.activation(w[:, h, :], xc[q][:, h, i:i + CH], ACT.Identity,
                                                            bias=V("conv_b", h) if i == 0 else 0.0,
                                                            scale=V("conv_w", h * TAPS + i))
                            last.then_inc(tap_ready, 1)
                        nc.scalar.activation(xc[1 - q][:, :, 0:HALO], xc[q][:, :, CH:CH + HALO], ACT.Copy).then_inc(halo_ready, 1)
                    if s == 7:
                        for h in range(HV):
                            written(f"z{h}")
                            nc.scalar.activation(sz[q][:, h, :], shared[:, :], ACT.Copy).then_inc(shared_read, 1)
                    if s == 9:
                        act.wait_ge(conv_ready, k)
                        nc.scalar.activation(u[q], wd, ACT.Silu).then_inc(u_ready, 1)
                        act.wait_ge(shared_read, shared_index("z1", k, pre, post) + 1)
                        nc.scalar.activation(sz[q], sz[q], ACT.Silu).then_inc(sz_ready, 1)
                        nc.scalar.activation(table_pad[:, :], ones_w[:, 0:1], ACT.Ln)
                    if s == 11:
                        written("dbc")
                        nc.scalar.activation(dbc[0:XPW, :], shared[0:XPW, :], ACT.Copy).then_inc(shared_read, 1)
                        act.wait_ge(shared_read, shared_index("dbc", k, pre, post) + 1)
                        nc.scalar.activation(bc_parts[q][:, :], dbc[0:PARTS * BC, :], ACT.Copy).then_inc(high_ready, 1)
                    if s == 12:
                        act.wait_ge(r1_ready, k)
                        nc.scalar.activation(bc_mid[:, :], r1[0:PARTS * BC, :], ACT.Copy).then_inc(mid_rounded, 1)
                        for h in range(HV):
                            written(f"dt{h}")
                            nc.scalar.activation(wa[:, h, :], shared[:, :], ACT.Relu, bias=V("b_dt", h)).then_inc(pos_dt, 1)
                            nc.scalar.activation(wb[:, h, :], shared[:, :], ACT.Abs, bias=V("b_dt", h)).then_inc(shared_read, 1)
                    if s == 13:
                        act.wait_ge(mid_rounded, k)
                        nc.scalar.activation(bc_parts[q][BC:2 * BC, :], bc_mid[BC:2 * BC, :], ACT.Copy).then_inc(mid_ready, 1)
                        act.wait_ge(shared_read, shared_index("dt1", k, pre, post) + 1)
                        nc.scalar.activation(wb, wb, ACT.Exp, scale=-1.0).then_inc(exp_dt, 1)
                        act.wait_ge(exp_dt, k)
                        nc.scalar.activation(wc, wb, ACT.Identity, bias=1.0).then_inc(one_dt, 1)
                        act.wait_ge(one_dt, k)
                        nc.scalar.activation(wd, wc, ACT.Ln).then_inc(log_dt, 1)
                        act.wait_ge(log_dt, k)
                        nc.scalar.activation(wc, wc, ACT.Identity, bias=minus1[:, :]).then_inc(less_dt, 1)

                def post_part(s):
                    if s == 0:
                        for h in range(HV):
                            last = nc.scalar.activation(yv[:, h, :], u[q][:, h, :], ACT.Copy, scale=V("d_skip", h))
                        last.then_inc(skip_ready, 1)
                    if s == 4:
                        act.wait_ge(shared_read, shared_index("out", k, pre, post) + 1)
                        act.dma_start(x1_dram[k - 3], x1c).then_inc(x1_stored, 16)
                    if s == 6:
                        act.wait_ge(shared_read, shared_index("pmean", k, pre, post) + 1)
                        nc.scalar.activation(psq, xd, ACT.Square).then_inc(psq_ready, 1)
                    if s == 8:
                        written("pvar")
                        nc.scalar.activation(prs, shared[:, :], ACT.Ln, bias=eps[:, :]).then_inc(shared_read, 1)
                        act.wait_ge(shared_read, shared_index("pvar", k, pre, post) + 1)
                        nc.scalar.activation(prs, prs, ACT.Exp, scale=-0.5).then_inc(prstd_ready, 1)
                    if s == 12:
                        act.wait_ge(xl_ready, k - 2)
                        act.dma_start(xl_dram[k - 3], xlc).then_inc(xl_stored, 16)

                for s in range(16):
                    if pre and s == 0:
                        act.wait_ge(adj_used, PIECES * k)
                        nc.scalar.activation(m1, mixed[:, :], ACT.Copy).then_inc(mixed_copied, 1)
                    if scan:
                        if s == 0:
                            act.wait_ge(dt_ready, cs + 1)
                        for h in range(HV):
                            wait(act, scan_done, HV * DS * cs + (HV * (s - 1) + h + 1))
                            nc.scalar.activation(da[h][:, :], dt[par][:, h, :], ACT.Exp,
                                                 scale=a_neg[:, h * DS + s:h * DS + s + 1]).then_inc(da_ready, 1)
                    if pre:
                        pre_part(s)
                    if post:
                        post_part(s)

            iterations(act, step)

            act.wait_ge(lstm_init, 2)
            nc.scalar.activation(table_pad[:, :], ones_w[:, 0:1], ACT.Sigmoid)
            pass_no = act.alloc_register("act_pass")
            go_on = act.alloc_register("act_go")
            act.reg_mov(pass_no, 0)
            act.reg_mov(go_on, 1)
            with act.While(lambda: act.snap(go_on)):
                pn = act.snap(pass_no)
                with act.Fori(0, SEG - 1, 2) as t:
                    for e in range(2):
                        for b in range(2):
                            done = 2 * SEG * pn + 2 * t + (2 * e + b + 1)
                            g = gates[b][e]
                            act.wait_ge(gates_ready, done)
                            nc.scalar.activation(tg[b], g[:, 3 * HS:4 * HS], ACT.Tanh).then_inc(tg_ready, 1)
                            nc.scalar.activation(sg[b], g[:, 0:3 * HS], ACT.Sigmoid).then_inc(sg_ready, 1)
                            act.wait_ge(cell_ready, done)
                            nc.scalar.activation(tc[b], c_st[:, b * HS:(b + 1) * HS], ACT.Tanh).then_inc(tc_ready, 1)
                act.wait_ge(flag_ready, pn + 1)
                act.sem_inc(flag_seen, 1)
                act.reg_load(go_on, flag[0:1, 0:1])
                act.reg_add(pass_no, pass_no, 1)

            def chunk(i, q):
                act.wait_ge(l0_ready, i + 1)
                wait(act, gsel_ready, i - 1)
                nc.scalar.activation(l0b[q], l_bank[0][q][:, :], ACT.Identity, bias=V("b_lin", 0)).then_inc(l0b_ready, 1)
                wait(act, dbl_ready, i - 1)
                nc.scalar.activation(h2[q].rearrange("p (s t) -> p t s", s=SPC),
                                     hs[:, 1:SEG + 1, bass.ds(i * SPC, SPC)], ACT.Copy, scale=2.0).then_inc(h2_ready, 1)

            by_chunk(act, chunk)

        @block.gpsimd
        def _(pool):
            nc.gpsimd.memset(sel[:, :], 0.0).then_inc(sel_ready, 1)
            view = sel[:, :].rearrange("p (n m) -> p n m", m=P)
            for g in range(PARTS):
                pool.wait_ge(sel_ready, g + 1)
                nc.gpsimd.affine_select(out=view, in_=view, compare_op=ALU.not_equal, fill=1.0, base=-BC * g,
                                        pattern=[[-1, BC], [0, P]], channel_multiplier=1).then_inc(sel_ready, 1)
            pool.wait_ge(consts_in, 32)

            def step(k, par, adj, pre, scan, post):
                cs, q = k - 2, 1 - par

                def pre_part(s):
                    if s == 4:
                        pool.wait_ge(rstd_ready, k)
                        nc.gpsimd.tensor_tensor(out=ht, in0=ht, in1=rs, op=ALU.mult).then_inc(hn_ready, 1)
                    if s == 7:
                        for i in range(1, TAPS):
                            pool.wait_ge(tap_ready, TAPS * (k - 1) + i + 1)
                            if i > 1:
                                pool.wait_ge(tap_done, (TAPS - 2) * (k - 1) + (i - 1))
                            nc.gpsimd.tensor_tensor(out=wd, in0=wd, in1=taps[i], op=ALU.add).then_inc(
                                tap_done if i < TAPS - 1 else conv_ready, 1)
                    if s == 14:
                        pool.wait_ge(less_dt, k)
                        nc.gpsimd.tensor_tensor(out=wb, in0=wc, in1=wb, op=ALU.subtract).then_inc(rem_dt, 1)
                        pool.wait_ge(rem_dt, k)
                        nc.gpsimd.tensor_tensor(out=wb, in0=wd, in1=wb, op=ALU.subtract).then_inc(sum_dt, 1)
                        pool.wait_ge(sum_dt, k)
                        pool.wait_ge(pos_dt, HV * k)
                        nc.gpsimd.tensor_tensor(out=dt[q], in0=wa, in1=wb, op=ALU.add).then_inc(dt_ready, 1)
                        pool.wait_ge(dt_ready, k)
                        nc.gpsimd.tensor_tensor(out=dtu[q], in0=dt[q], in1=u[q], op=ALU.mult).then_inc(dtu_ready, 1)

                def post_part(s):
                    if s == 0:
                        pool.wait_ge(y_added, (DS - 1) * (k - 2))
                        pool.wait_ge(skip_ready, k - 2)
                        nc.gpsimd.tensor_tensor(out=yv, in0=yv, in1=acc, op=ALU.add).then_inc(y_skip, 1)
                        pool.wait_ge(y_skip, k - 2)
                        nc.gpsimd.tensor_tensor(out=yv, in0=yv, in1=sz[q], op=ALU.mult).then_inc(y_ready, 1)
                    if s == 9:
                        pool.wait_ge(prstd_ready, k - 2)
                        wait(pool, xl_stored, 16 * (k - 3))
                        nc.gpsimd.tensor_tensor(out=xlc.rearrange("p (t s) -> p s t", s=SPC),
                                                in0=xd.rearrange("p (s t) -> p s t", s=SPC),
                                                in1=prs.rearrange("p (s t) -> p s t", s=SPC),
                                                op=ALU.mult).then_inc(xl_ready, 1)

                def add(n):
                    pool.wait_ge(hc_done, DS * cs + n + 1)
                    if n > 1:
                        pool.wait_ge(y_added, (DS - 1) * cs + (n - 1))
                    nc.gpsimd.tensor_tensor(out=acc, in0=hc[0] if n == 1 else acc, in1=hc[n % 2],
                                            op=ALU.add).then_inc(y_added, 1)

                for s in range(16):
                    if post and s == 0:
                        post_part(s)
                    if scan and s >= 2:
                        add(s - 1)
                    if pre:
                        pre_part(s)
                    if post and s > 0:
                        post_part(s)
                if scan:
                    add(DS - 1)

            iterations(pool, step)

            pool.wait_ge(lstm_init, 3)
            def chunk(i, q):
                pool.wait_ge(x1f_in[q], 8 * (i - q) + 16)
                pool.wait_ge(h2_ready, i + 1)
                nc.gpsimd.tensor_tensor(out=fin_all[:, bass.ds(i * CH, CH)], in0=h2[q], in1=x1f[q], op=ALU.add).then_inc(dbl_ready, 1)

            by_chunk(pool, chunk)

        @block.vector
        def _(dve):
            nc.vector.memset(mean_w[:, :], 1.0 / D)
            nc.vector.memset(eps[:, :], EPS)
            nc.vector.memset(minus1[:, :], -1.0)
            nc.vector.memset(hstate[:, :], 0.0)
            nc.vector.memset(xc[0][:, :, 0:HALO], 0.0).then_inc(halo_ready, 1)
            nc.vector.memset(ones_w[:, :], 1.0).then_inc(consts_ready, 1)
            dve.wait_ge(x_in, 16)
            for g in range(4):
                blk = slice(16 * g, 16 * g + 16)
                xg = xn[:, blk, :]

                def spread(k):
                    return stat[:, k, blk].unsqueeze(2).broadcast_to([P, 16, D])

                nc.vector.reduce_sum(stat[:, 0, blk], xg, axis=AX.X).then_inc(row_sum, 1)
                dve.wait_ge(row_sum, g + 1)
                nc.vector.tensor_scalar(stat[:, 0, blk], stat[:, 0, blk], 1.0 / D, None, ALU.mult).then_inc(row_mean, 1)
                dve.wait_ge(row_mean, g + 1)
                nc.vector.tensor_tensor(out=xg, in0=xg, in1=spread(0), op=ALU.subtract).then_inc(row_centred, 1)
                dve.wait_ge(row_sq, g + 1)
                nc.vector.reduce_sum(stat[:, 1, blk], sq_rows, axis=AX.X).then_inc(row_var, 1)
                dve.wait_ge(row_rstd, g + 1)
                nc.vector.tensor_tensor(out=xg, in0=xg, in1=spread(3), op=ALU.mult).then_inc(xn_ready, 1)
            dve.wait_ge(init_done, 1)
            nc.vector.tensor_scalar(a_neg[:, :], a_neg[:, :], -1.0, None, ALU.mult).then_inc(init_done, 1)
            nc.vector.tensor_scalar(negbw[:, :], V("bw"), -1.0, None, ALU.mult)
            nc.vector.memset(bias_w[:, :], 0.0).then_inc(bias_ready, 1)
            dve.wait_ge(bias_loaded, 48)
            n = [0]

            def link(ins):
                n[0] += 1
                ins.then_inc(check_step, 1)
                dve.wait_ge(check_step, n[0])

            full, tail = bias_in[:, 0:P], bias_in[:, P:2 * P]
            for i in range(PARTS):
                r = slice(32 * i, 32 * i + 4)
                link(nc.vector.tensor_tensor(out=full[r], in0=full[r], in1=tail[r], op=ALU.add))
                link(nc.vector.tensor_copy(bias_mid[r, :], full[r]))
                for _ in range(i):
                    link(nc.vector.tensor_tensor(out=full[r], in0=full[r], in1=bias_mid[r, :], op=ALU.subtract))
                    link(nc.vector.tensor_copy(bias_mid[r, :], full[r]))
                if i == 0:
                    dve.wait_ge(bias_ready, 1)
                link(nc.vector.tensor_copy(bias_w[r, :], bias_mid[r, :]))
            dve.sem_inc(bias_ready, 1)
            bias_links = n[0]

            def step(k, par, adj, pre, scan, post):
                cs, q = k - 2, 1 - par

                def written(name):
                    dve.wait_ge(shared_written, shared_index(name, k, pre, post) + 1)

                def side_part(s):
                    if pre and s == 2:
                        written("mean")
                        nc.vector.tensor_tensor(out=ht, in0=ht, in1=shared[:, :], op=ALU.subtract).then_inc(shared_read, 1)
                    if post and s == 3:
                        written("out")
                        dve.wait_ge(xt_in[q], 8 * (k - 3 - q) + 16)
                        wait(dve, x1_stored, 16 * (k - 3))
                        nc.vector.tensor_tensor(out=x1c, in0=xt[q], in1=shared[:, :], op=ALU.add).then_inc(shared_read, 1)
                    if post and s == 5:
                        written("pmean")
                        nc.vector.tensor_tensor(out=xd, in0=x1c, in1=shared[:, :], op=ALU.subtract).then_inc(shared_read, 1)
                    if pre and s == 11:
                        dve.wait_ge(high_ready, k)
                        nc.vector.tensor_tensor(out=r1[0:PARTS * BC, :], in0=dbc[0:PARTS * BC, :], in1=bc_parts[q][:, :],
                                                op=ALU.subtract).then_inc(r1_ready, 1)
                    if pre and s == 12:
                        dve.wait_ge(mid_rounded, k)
                        nc.vector.tensor_tensor(out=bc_parts[q][2 * BC:3 * BC, :], in0=r1[2 * BC:3 * BC, :],
                                                in1=bc_mid[2 * BC:3 * BC, :], op=ALU.subtract).then_inc(low_ready, 1)

                def both(ap):
                    return ap[:, :].unsqueeze(1).broadcast_to([P, HV, CH])

                def make_dbu(n):
                    dve.wait_ge(b_ready, DS * cs + n + 1)
                    wait(dve, scan_done, HV * (DS * cs + n - 1) if isinstance(cs, int) else HV * DS * cs + HV * (n - 1))
                    nc.vector.tensor_tensor(out=dbu[n % 2], in0=dtu[par], in1=both(b_bank[n % 2]),
                                            op=ALU.mult).then_inc(dbu_done, 1)

                def make_hc(n):
                    dve.wait_ge(c_ready, DS * cs + n + 1)
                    dve.wait_ge(scan_done, HV * DS * cs + HV * (n + 1))
                    wait(dve, y_added, (DS - 1) * cs + (max(n - 2, 1) if n >= 2 else n - 1))
                    nc.vector.tensor_tensor(out=hc[n % 2], in0=hb[n % 2], in1=both(c_bank[n % 2]),
                                            op=ALU.mult).then_inc(hc_done, 1)
                    nc.vector.tensor_copy(hstate[:, HV * n:HV * n + HV], hb[n % 2][:, :, CH - 1]).then_inc(state_saved, 1)

                for s in range(16):
                    side_part(s)
                    if not scan:
                        continue
                    if s == 0:
                        dve.wait_ge(dtu_ready, cs + 1)
                        make_dbu(0)
                    if s < DS - 1:
                        make_dbu(s + 1)
                    for h in range(HV):
                        dve.wait_ge(da_ready, HV * DS * cs + (HV * s + h + 1))
                        if h == 0:
                            dve.wait_ge(dbu_done, DS * cs + s + 1)
                            wait(dve, state_saved, DS * cs + (s - 1))
                            wait(dve, hc_done, DS * cs + (s - 1))
                        nc.vector.tensor_tensor_scan(hb[s % 2][:, h, :], da[h][:, :], dbu[s % 2][:, h, :],
                                                     hstate[:, HV * s + h:HV * s + h + 1],
                                                     ALU.mult, ALU.add).then_inc(scan_done, 1)
                    if s >= 1:
                        make_hc(s - 1)
                if scan:
                    make_hc(DS - 1)

            iterations(dve, step)

            dve.wait_ge(x1_stored, 16 * NC)
            dve.wait_ge(xl_stored, 16 * NC)
            dve.wait_ge(adj_used, PIECES * NC)
            nc.vector.memset(hs[:, 0, :], 0.0)
            nc.vector.memset(c_in, 0.0)
            nc.vector.memset(passes, 0.0)
            nc.vector.memset(run_total, 0.0)
            nc.vector.memset(c_st, 0.0).then_inc(lstm_init, 1)
            dve.wait_ge(lstm_init, 1)
            for l in range(2):
                last = nc.vector.tensor_copy(wlin[:, l * P:(l + 1) * P], V("w_lin", l).broadcast_to([P, P]))
            last.then_inc(lstm_init, 1)
            pass_no = dve.alloc_register("dve_pass")
            go_on = dve.alloc_register("dve_go")
            dve.reg_mov(pass_no, 0)
            dve.reg_mov(go_on, 1)
            checks = 8
            with dve.While(lambda: dve.snap(go_on)):
                pn = dve.snap(pass_no)
                with dve.Fori(0, SEG) as t:
                    for b in range(2):
                        seg = slice(b * HS, (b + 1) * HS)
                        done = 2 * SEG * pn + 2 * t + (b + 1)
                        dve.wait_ge(sg_ready, done)
                        nc.vector.tensor_tensor(out=fc[b], in0=sg[b][:, HS:2 * HS], in1=c_st[:, seg], op=ALU.mult).then_inc(fc_ready, 1)
                        dve.wait_ge(tg_ready, done)
                        nc.vector.tensor_tensor(out=ig[b], in0=sg[b][:, 0:HS], in1=tg[b], op=ALU.mult).then_inc(ig_ready, 1)
                        dve.wait_ge(fc_ready, done)
                        dve.wait_ge(ig_ready, done)
                        nc.vector.tensor_tensor(out=c_st[:, seg], in0=fc[b], in1=ig[b], op=ALU.add).then_inc(cell_ready, 1)
                        dve.wait_ge(tc_ready, done)
                        nc.vector.tensor_tensor(out=hs[:, t + 1, seg], in0=sg[b][:, 2 * HS:3 * HS], in1=tc[b],
                                                op=ALU.mult).then_inc(hid_ready, 1)
                base = checks * pn + bias_links
                k = [0]

                def then(ins):
                    k[0] += 1
                    ins.then_inc(check_step, 1)
                    dve.wait_ge(check_step, base + k[0])

                dve.wait_ge(hid_ready, 2 * SEG * pn + 2 * SEG)
                E = NSEG - 1
                nc.vector.tensor_tensor(out=diff[:, 0:E], in0=hs[:, SEG, 0:E], in1=hs[:, 0, 1:NSEG], op=ALU.subtract)
                nc.vector.tensor_scalar(passes, passes, 1.0, None, ALU.add)
                then(nc.vector.tensor_tensor(out=diff[:, E:2 * E], in0=c_st[:, 0:E], in1=c_in[:, 1:NSEG], op=ALU.subtract))
                nc.vector.tensor_copy(hs[:, 0, 1:NSEG], hs[:, SEG, 0:E])
                nc.vector.tensor_copy(c_in[:, 1:NSEG], c_st[:, 0:E])
                then(nc.vector.tensor_tensor(out=diff, in0=diff, in1=diff, op=ALU.mult))
                then(nc.vector.tensor_scalar(diff, diff, TOL * TOL, None, ALU.is_le))
                then(nc.vector.tensor_scalar(alive, passes, float(NSEG), None, ALU.is_lt))
                nc.vector.reduce_sum(agree, diff, axis=AX.X).then_inc(agree_ready, 1)
                then(nc.vector.tensor_copy(c_st, c_in))
                dve.wait_ge(agree_sum, pn + 1)
                nc.vector.scalar_tensor_tensor(out=flag[:, :], in0=count_ps[0:1, 0:1], scalar=float(2 * E * P),
                                               in1=alive[0:1, :], op0=ALU.is_lt, op1=ALU.mult).then_inc(flag_ready, 1)
                dve.wait_ge(flag_ready, pn + 1)
                dve.sem_inc(flag_seen, 1)
                dve.reg_load(go_on, flag[0:1, 0:1])
                for _ in range(checks - k[0]):
                    dve.sem_inc(check_step, 1)
                dve.reg_add(pass_no, pass_no, 1)
            dve.sem_inc(lstm_init, 1)

            def chunk(i, q):
                t0 = i * CH
                dve.wait_ge(l1_ready, i + 1)
                dve.wait_ge(l0b_ready, i + 1)
                wait(dve, wsel_ready, i - 1)
                nc.vector.scalar_tensor_tensor(out=gsel[q], in0=l_bank[1][q][:, :], scalar=V("b_lin", 1), in1=l0b[q],
                                               op0=ALU.add, op1=ALU.is_gt).then_inc(gsel_ready, 1)
                dve.wait_ge(gsel_ready, i + 1)
                wait(dve, pre_ready, i - 1)
                nc.vector.tensor_tensor(out=wsel[q].rearrange("p (s t) -> p t s", s=SPC),
                                        in0=gsel[q].rearrange("p (t s) -> p t s", s=SPC),
                                        in1=hs[:, 1:SEG + 1, bass.ds(i * SPC, SPC)], op=ALU.mult).then_inc(wsel_ready, 1)
                dve.wait_ge(wsel_ready, i + 1)
                wait(dve, inc_ready, i)
                nc.vector.tensor_tensor_scan(inc_all[:, bass.ds(t0, CH)], wsel[q], wsel[q], run_total,
                                             ALU.add, ALU.bypass).then_inc(inc_ready, 1)
                dve.wait_ge(inc_ready, i + 1)
                nc.vector.tensor_copy(run_total, inc_all[:, bass.ds(t0 + (CH - 1), 1)])
                nc.vector.tensor_tensor(out=wsel[q], in0=inc_all[:, bass.ds(t0, CH)], in1=wsel[q],
                                        op=ALU.subtract).then_inc(pre_ready, 1)
                dve.wait_ge(pre_ready, i + 1)
                dve.wait_ge(dbl_ready, i + 1)
                nc.vector.scalar_tensor_tensor(out=fin_all[:, bass.ds(t0, CH)], in0=wsel[q], scalar=V("fw"),
                                               in1=fin_all[:, bass.ds(t0, CH)], op0=ALU.mult, op1=ALU.add).then_inc(fwd_done, 1)

            by_chunk(dve, chunk)
            def chunk(i, q):
                t0 = i * CH
                nc.vector.tensor_scalar(inc_all[:, bass.ds(t0, CH)], inc_all[:, bass.ds(t0, CH)], run_total, negbw[:, :],
                                        ALU.subtract, ALU.mult).then_inc(suf_ready, 1)
                dve.wait_ge(suf_ready, i + 1)
                wait(dve, out_done[q], 8 * (i - q))
                nc.vector.tensor_tensor(out=ob[q], in0=inc_all[:, bass.ds(t0, CH)], in1=fin_all[:, bass.ds(t0, CH)],
                                        op=ALU.add).then_inc(ob_ready, 1)

            by_chunk(dve, chunk)


_INS = ["adj_t", "x_rows", "x_t", "weights", "vectors", "lstm_bias"]


def kernel(**inputs):
    import concourse.bacc as bacc
    from concourse.bass_utils import run_bass_kernel_spmd

    a = {k: np.asarray(v) for k, v in inputs.items()}
    g, f = "L0_gnn_", "L0_ffn_"
    x, adj = a["x"], a["adj"]

    def gate_columns(w):
        w = w.T.reshape(D, 4, D)
        return np.concatenate([w[:, 0], w[:, 1], w[:, 3], w[:, 2]], axis=1)

    def by_half(v):
        v = v.reshape(HV, P, -1)
        return np.concatenate([v[h] for h in range(HV)], axis=1)

    w_xp = a[g + "w_xp"]
    w_xp = np.concatenate([w_xp[:, DR:]] * PARTS + [w_xp[:, :DR]], axis=1)
    w_dt = np.zeros((P, DI), np.float32)
    w_dt[PARTS * BC:XPW] = a[g + "w_dt"]
    weights = np.concatenate([a[g + "gcn_w"], a[g + "w_in"], by_half(w_xp), w_dt, by_half(a[g + "w_out"]),
                              gate_columns(a[f + "W_ih"]), gate_columns(a[f + "W_hh"])], axis=1)

    def col(v):
        return v.reshape(P, 1)

    vectors = np.concatenate([col(a[g + "gcn_b"]), col(a[g + "ln_g"]), col(a[g + "ln_b"]), by_half(a[g + "conv_b"]),
                              by_half(a[g + "conv_w"]), by_half(a[g + "b_dt"]), by_half(a[g + "D_skip"]),
                              col(a[f + "fw_att"]), col(a[f + "bw_att"]), by_half(a[g + "A_log"]),
                              a[f + "W_lin"].T, np.broadcast_to(a[f + "b_lin"], (P, 2))], axis=1)

    def gate_rows(b):
        b = b.reshape(4, D)
        return b[[0, 1, 3, 2]]

    arrays = dict(
        adj_t=adj.reshape(NC, CH, P, BLK).transpose(0, 2, 3, 1).reshape(NC, P, BLK * CH),
        x_rows=x.reshape(P, BLK * D),
        x_t=x.reshape(NC, CH, D).transpose(0, 2, 1),
        weights=weights, vectors=vectors,
        lstm_bias=np.concatenate([gate_rows(a[f + "b_ih"]), gate_rows(a[f + "b_hh"])], axis=1),
    )
    arrays = {k: np.ascontiguousarray(v) for k, v in arrays.items()}
    nc = bacc.Bacc("TRN2", target_bir_lowering=False, num_devices=1)
    args = [nc.dram_tensor(n, arrays[n].shape, mybir.dt.from_np(arrays[n].dtype), kind="ExternalInput").ap() for n in _INS]
    out = nc.dram_tensor("out_t", (NC, P, CH), mybir.dt.float32, kind="ExternalOutput").ap()
    build(nc, *args, out)
    r = run_bass_kernel_spmd(nc, [arrays], core_ids=[0])
    return np.ascontiguousarray(r.results[0]["out_t"].transpose(0, 2, 1).reshape(N, D))
```

```python
from contextlib import ExitStack

import numpy as np

import concourse.bass as bass
from concourse import mybir

N = 8192
D = 128
P = 128
CH = 512
NC = N // CH
BLK = N // P
PB = 4
PIECES = BLK // PB
RING = 4
DI = 256
HV = DI // P
DS = 16
TAPS = 4
HALO = TAPS - 1
DR = 8
BC = 2 * DS
XPW = 3 * BC + DR
SEG = 32
WARM = 32
NSEG = N // SEG
SPC = CH // SEG
HS = NSEG // 2
EPS = 1e-5
TOL = 2.0 ** -21
LN_EXP = "natural_log_exp_and_others"
PARTS = 3

WSIZE = dict(gcn=D, w_in=2 * DI, w_xp=HV * XPW, w_dt=DI, w_out=HV * D, w_ih=4 * D, w_hh=4 * D)
WOFF, _o = {}, 0
for _n, _s in WSIZE.items():
    WOFF[_n] = _o
    _o += _s
WTOT = _o
VSIZE = dict(gcn_b=1, ln_g=1, ln_b=1, conv_b=HV, conv_w=HV * TAPS, b_dt=HV, d_skip=HV, fw=1, bw=1,
             a_log=HV * DS, w_lin=2, b_lin=2)
VOFF, _o = {}, 0
for _n, _s in VSIZE.items():
    VOFF[_n] = _o
    _o += _s
VTOT = _o

SHARED = [("gcn", 0, "pre"), ("mean", 1, "pre"), ("var", 2, "pre"), ("out", 3, "post"),
          ("pmean", 4, "post"), ("xc0", 5, "pre"), ("xc1", 5.5, "pre"), ("z0", 6, "pre"),
          ("z1", 6.5, "pre"), ("pvar", 7, "post"), ("dbc", 9, "pre"), ("dt0", 10, "pre"),
          ("dt1", 10.5, "pre")]
PRE_STEPS = sum(s[2] == "pre" for s in SHARED)
POST_STEPS = sum(s[2] == "post" for s in SHARED)


def shared_index(step, k, pre, post):
    if isinstance(k, int):
        before = PRE_STEPS * (min(k, NC + 1) - 1) + POST_STEPS * max(0, k - 3)
    else:
        before = (PRE_STEPS + POST_STEPS) * k - (PRE_STEPS + 3 * POST_STEPS)
    names = [s[0] for s in SHARED if (pre and s[2] == "pre") or (post and s[2] == "post")]
    return before + names.index(step)


def wait(eng, sem, value):
    if not (isinstance(value, int) and value <= 0):
        eng.wait_ge(sem, value)


def build(nc, adj_t, x_rows, x_t, weights, vectors, lstm_bias, out_t):
    F32, BF, I32 = mybir.dt.float32, mybir.dt.bfloat16, mybir.dt.int32
    ALU, ACT, AX = mybir.AluOpType, mybir.ActivationFunctionType, mybir.AxisListType

    x1_dram = nc.dram_tensor("x1_scratch", (NC, P, CH), F32, kind="Internal").ap()
    xl_dram = nc.dram_tensor("xl_scratch", (NC, P, CH), F32, kind="Internal").ap()

    ctx = ExitStack()
    with ctx:
        def sb(name, shape, dt=F32):
            return ctx.enter_context(nc.sbuf_tensor(name, shape, dt))

        def sem(name):
            return ctx.enter_context(nc.semaphore(name))

        xh = sb("xh", [P, (SEG + 1) * NSEG])
        xn = xh[:, 0:N].rearrange("p (b d) -> p b d", d=D)
        hs = xh[:, :].rearrange("p (t s) -> p t s", s=NSEG)
        ring = sb("ring", [P, RING * PB * CH])
        xls = ring[:, :].rearrange("p (c t) -> p c t", c=NC)
        w_sb = sb("w_sb", [P, WTOT])
        v_sb = sb("v_sb", [P, VTOT])
        sel = sb("sel", [PARTS * BC, BC * P], BF)
        mean_w = sb("mean_w", [P, P])
        ones_w = sb("ones_w", [P, P])
        eps = sb("eps", [P, 1])
        a_neg = sb("a_neg", [P, HV * DS])
        negbw = sb("negbw", [P, 1])
        bc_parts = [sb(f"bc_parts{i}", [PARTS * BC, CH], BF) for i in range(2)]
        bc_mid = sb("bc_mid", [PARTS * BC, CH], BF)
        hstate = sb("hstate", [P, DS * HV])
        bias_in = sb("bias_in", [PARTS * BC, 2 * P])
        bias_mid = sb("bias_mid", [PARTS * BC, P], BF)
        bias_w = sb("bias_w", [PARTS * BC, P], BF)
        flag = sb("flag", [1, 1], I32)
        run_total = sb("run_total", [P, 1])[:, :]

        WORK = 29 * 1024 + 512
        work = sb("work", [P, WORK])
        at = [0]

        def carve(n):
            a = at[0]
            at[0] += n
            assert at[0] <= WORK, at[0]
            return work[:, a:a + n]

        def halves(ap):
            return ap.rearrange("p (h t) -> p h t", h=HV)

        W2 = HV * CH
        dbu = [halves(carve(W2)) for _ in range(2)]
        hb = [halves(carve(W2)) for _ in range(2)]
        hc = [halves(carve(W2)) for _ in range(2)]
        xc = [halves(carve(HV * (HALO + CH + 1))) for _ in range(2)]
        u = [halves(carve(W2)) for _ in range(2)]
        sz = [halves(carve(W2)) for _ in range(2)]
        dt = [halves(carve(W2)) for _ in range(2)]
        dtu = [halves(carve(W2)) for _ in range(2)]
        acc = halves(carve(W2))
        yv = halves(carve(W2))
        wa, wb, wc, wd = (halves(carve(W2)) for _ in range(4))
        m1, ht, sq, rs = (carve(CH) for _ in range(4))
        dbc, r1 = carve(CH), carve(CH)
        xt = [carve(CH) for _ in range(2)]
        x1c, xd, psq, prs = (carve(CH) for _ in range(4))
        xlc = carve(CH)
        sq_rows = work[:, 0:16 * D].rearrange("p (b d) -> p b d", d=D)
        stat = work[:, 4096:4096 + 4 * BLK].rearrange("p (k b) -> p k b", k=4)
        at[0] = 0
        inc_all = carve(N)
        fin_all = carve(N)
        c_in = carve(NSEG)
        c_st = carve(NSEG)
        sg = [carve(3 * HS) for _ in range(2)]
        tg = [carve(HS) for _ in range(2)]
        fc = [carve(HS) for _ in range(2)]
        ig = [carve(HS) for _ in range(2)]
        tc = [carve(HS) for _ in range(2)]
        diff = carve(2 * (NSEG - 1))
        agree = carve(1)
        alive = carve(1)
        passes = carve(1)
        wlin = carve(2 * P)
        l0b = [carve(CH) for _ in range(2)]
        gsel = [carve(CH) for _ in range(2)]
        wsel = [carve(CH) for _ in range(2)]
        x1f = [carve(CH) for _ in range(2)]
        ob = [carve(CH) for _ in range(2)]
        h2 = [carve(CH) for _ in range(2)]
        prefix = [carve(CH) for _ in range(2)]

        bias_cols = sel[:, :].rearrange("p (n m) -> p n m", m=P)[:, 0:4, 0:HS]

        def W(name, lo=0, hi=None):
            o = WOFF[name]
            return w_sb[:, o + lo:o + (WSIZE[name] if hi is None else hi)]

        def V(name, i=0):
            return v_sb[:, VOFF[name] + i:VOFF[name] + i + 1]

        bank = [ctx.enter_context(nc.psum_tensor(f"bank{i}", [P, CH], F32)) for i in range(8)]
        mixed, shared = bank[0], bank[2]
        da = [bank[1], bank[7]]
        b_bank = [bank[3], bank[4]]
        c_bank = [bank[5], bank[6]]
        gates = [[bank[0], bank[1]], [bank[2], bank[3]]]
        count_ps = bank[4]
        l_bank = [[bank[0], bank[1]], [bank[2], bank[3]]]

        consts_in, bias_loaded = sem("consts_in"), sem("bias_loaded")
        x_in = [sem(f"x_in{i}") for i in range(4)]
        consts_ready, sel_ready, init_done = sem("consts_ready"), sem("sel_ready"), sem("init_done")
        row_sum, row_mean, row_centred, row_sq = sem("row_sum"), sem("row_mean"), sem("row_centred"), sem("row_sq")
        row_var, row_ln, row_rstd, xn_ready = sem("row_var"), sem("row_ln"), sem("row_rstd"), sem("xn_ready")
        adj_in = [sem(f"adj_in{i}") for i in range(RING)]
        adj_used = sem("adj_used")
        mixed_copied = sem("mixed_copied")
        shared_written, shared_read = sem("shared_written"), sem("shared_read")
        squared = sem("squared")
        lnv_ready, rstd_ready, hn_ready, h_ready = sem("lnv_ready"), sem("rstd_ready"), sem("hn_ready"), sem("h_ready")
        tap_ready, tap_done = sem("tap_ready"), sem("tap_done")
        halo_ready = sem("halo_ready")
        z_raw, u_ready, sz_ready = sem("z_raw"), sem("u_ready"), sem("sz_ready")
        high_ready, r1_ready = sem("high_ready"), sem("r1_ready")
        mid_rounded, mid_ready, low_ready = sem("mid_rounded"), sem("mid_ready"), sem("low_ready")
        pos_dt, exp_dt, one_dt, log_dt = (sem(f"{n}_dt") for n in ("pos", "exp", "one", "log"))
        rem_dt, sum_dt, dt_ready, dtu_ready = sem("rem_dt"), sem("sum_dt"), sem("dt_ready"), sem("dtu_ready")
        b_ready, c_ready, da_ready = sem("b_ready"), sem("c_ready"), sem("da_ready")
        dbu_done, scan_done, hc_done, state_saved = sem("dbu_done"), sem("scan_done"), sem("hc_done"), sem("state_saved")
        y_added, skip_ready, y_skip, y_ready = (sem(n) for n in ("y_added", "skip_ready", "y_skip", "y_ready"))
        xt_in, x1_stored = [sem(f"xt_in{i}") for i in range(2)], sem("x1_stored")
        psq_ready, plnv_ready, prstd_ready = sem("psq_ready"), sem("plnv_ready"), sem("prstd_ready")
        xl_ready, xl_stored = sem("xl_ready"), sem("xl_stored")
        xls_in, lstm_init = sem("xls_in"), sem("lstm_init")
        bias_ready, guess_ready = sem("bias_ready"), sem("guess_ready")
        gates_ready = sem("gates_ready")
        tg_ready, sg_ready, fc_ready, ig_ready = sem("tg_ready"), sem("sg_ready"), sem("fc_ready"), sem("ig_ready")
        cell_ready, tc_ready, hid_ready = sem("cell_ready"), sem("tc_ready"), sem("hid_ready")
        flag_seen = sem("flag_seen")
        agree_ready, agree_sum, flag_ready, check_step = sem("agree_ready"), sem("agree_sum"), sem("flag_ready"), sem("check_step")
        l0_ready, l1_ready, l0b_ready, gsel_ready = sem("l0_ready"), sem("l1_ready"), sem("l0b_ready"), sem("gsel_ready")
        wsel_ready, inc_ready, dbl_ready, h2_ready = sem("wsel_ready"), sem("inc_ready"), sem("dbl_ready"), sem("h2_ready")
        x1f_in, out_done = ([sem(f"{n}{i}") for i in range(2)] for n in ("x1f_in", "out_done"))
        total_ready, fwd_done, pre_ready, suf_ready, ob_ready = (sem(n) for n in ("total_ready", "fwd_done", "pre_ready", "suf_ready", "ob_ready"))

        block = ctx.enter_context(nc.Block())

        def iterations(eng, step):
            def flags(k):
                return k < NC, 1 <= k <= NC, 2 <= k <= NC + 1, 3 <= k <= NC + 2
            for k in range(4):
                step(k, k % 2, *flags(k))
            with eng.Fori(4, NC - 1, 2) as k:
                step(k, 0, True, True, True, True)
                step(k + 1, 1, True, True, True, True)
            for k in range(NC, NC + 3):
                step(k, k % 2, *flags(k))

        def by_chunk(eng, step):
            for c in range(2):
                step(c, c)
            with eng.Fori(2, NC - 1, 2) as c:
                step(c, 0)
                step(c + 1, 1)

        @block.sync
        def _(sp):
            for g in range(4):
                sp.dma_start(xh[:, g * 16 * D:(g + 1) * 16 * D], x_rows[:, g * 16 * D:(g + 1) * 16 * D]).then_inc(x_in[g], 16)
            sp.dma_start(w_sb[:, :], weights).then_inc(consts_in, 16)
            sp.dma_start(v_sb[:, :], vectors).then_inc(consts_in, 16)

            def step(k, par, adj, pre, scan, post):
                if post:
                    wait(sp, x1_stored, 16 * (k - 4))
                    sp.dma_start(xt[1 - par], x_t[k - 3]).then_inc(xt_in[1 - par], 16)
                if adj:
                    for j in range(PIECES):
                        r = j % RING
                        wait(sp, adj_used, PIECES * k + (j - RING + 1))
                        sp.dma_start(ring[:, r * PB * CH:(r + 1) * PB * CH],
                                     adj_t[k, :, j * PB * CH:(j + 1) * PB * CH]).then_inc(adj_in[r], 16)

            iterations(sp, step)
            sp.wait_ge(adj_used, PIECES * NC)
            sp.wait_ge(xl_stored, 16 * NC)
            sp.dma_start(xls, xl_dram.rearrange("c p t -> p c t")).then_inc(xls_in, 16)
            sp.wait_ge(x1_stored, 16 * NC)
            sp.wait_ge(prstd_ready, NC)
            def chunk(i, q):
                wait(sp, dbl_ready, i - 1)
                sp.dma_start(x1f[q], x1_dram[i]).then_inc(x1f_in[q], 16)

            by_chunk(sp, chunk)
            def chunk(i, q):
                sp.wait_ge(ob_ready, i + 1)
                sp.dma_start(out_t[i], ob[q]).then_inc(out_done[q], 16)

            by_chunk(sp, chunk)
            for q in range(2):
                sp.wait_ge(out_done[q], 8 * NC)

        @block.tensor
        def _(pe):
            pe.wait_ge(consts_in, 32)
            pe.wait_ge(consts_ready, 1)
            pe.wait_ge(sel_ready, 4)

            def step(k, par, adj, pre, scan, post):
                cs = k - 2

                def shared_step(name):
                    i = shared_index(name, k, pre, post)
                    wait(pe, shared_read, i)
                    out = shared[:, :]
                    if name == "gcn":
                        pe.wait_ge(mixed_copied, k)
                        ins = [(W("gcn"), m1)]
                    elif name == "mean":
                        ins = [(mean_w[:, :], ht)]
                    elif name == "var":
                        pe.wait_ge(squared, k)
                        ins = [(mean_w[:, :], sq)]
                    elif name in ("xc0", "xc1", "z0", "z1"):
                        b = ("xc0", "xc1", "z0", "z1").index(name)
                        pe.wait_ge(h_ready, k)
                        ins = [(W("w_in", b * P, (b + 1) * P), ht)]
                    elif name == "dbc":
                        pe.wait_ge(u_ready, k)
                        out = shared[0:XPW, :]
                        ins = [(W("w_xp", h * XPW, (h + 1) * XPW), u[1 - par][:, h, :]) for h in range(HV)]
                    elif name in ("dt0", "dt1"):
                        h = int(name[2])
                        o = WOFF["w_dt"] + h * P
                        ins = [(w_sb[0:XPW, o:o + P], dbc[0:XPW, :])]
                    elif name == "out":
                        pe.wait_ge(y_ready, k - 2)
                        ins = [(W("w_out", h * D, (h + 1) * D), yv[:, h, :]) for h in range(HV)]
                    elif name == "pmean":
                        ins = [(mean_w[:, :], x1c)]
                    else:
                        pe.wait_ge(psq_ready, k - 2)
                        ins = [(mean_w[:, :], psq)]
                    for n, (a, b) in enumerate(ins):
                        last = nc.tensor.matmul(out, a, b, start=(n == 0), stop=(n == len(ins) - 1))
                    last.then_inc(shared_written, 1)

                def spread(bank_, used, ready, row, n, c=cs, q=par):
                    wait(pe, used, DS * c + (n - 1))
                    nc.tensor.matmul(bank_[n % 2][:, :], sel[:, row * P:(row + 1) * P],
                                     bc_parts[q][:, :], start=True, stop=True).then_inc(ready, 1)

                def mid_slot(s):
                    shared_steps(s + 0.5)
                    if scan:
                        spread(c_bank, hc_done, c_ready, DS + s, s)
                    if pre and s == DS - 1:
                        pe.wait_ge(low_ready, k)
                        pe.wait_ge(mid_ready, k)
                        spread(b_bank, dbu_done, b_ready, 0, 0, k - 1, 1 - par)

                def shared_steps(at_slot):
                    for name, slot, stage in SHARED:
                        if slot == at_slot and ((stage == "pre" and pre) or (stage == "post" and post)):
                            shared_step(name)

                for s in range(16):
                    if scan:
                        if s < DS - 1:
                            spread(b_bank, dbu_done, b_ready, s + 1, s + 1)
                    shared_steps(s)
                    if adj:
                        if s == 0:
                            wait(pe, mixed_copied, k)
                        r = s % RING
                        if not scan:
                            if isinstance(k, int) and k == 0 and s % 4 == 0:
                                pe.wait_ge(xn_ready, s // 4 + 1)
                        pe.wait_ge(adj_in[r], 16 * (PIECES // RING) * k + 16 * (s // RING + 1))
                        for b in range(PB):
                            if b == PB // 2:
                                mid_slot(s)
                            j = s * PB + b
                            a = ring[:, (r * PB + b) * CH:(r * PB + b + 1) * CH]
                            last = nc.tensor.matmul(mixed[:, :], xn[:, j, :], a, start=(j == 0), stop=(j == BLK - 1))
                        last.then_inc(adj_used, 1)
                    else:
                        mid_slot(s)

            iterations(pe, step)

            pe.wait_ge(xls_in, 16)
            pe.wait_ge(bias_ready, 1)
            pe.wait_ge(lstm_init, 2)
            pass_no = pe.alloc_register("pe_pass")
            go_on = pe.alloc_register("pe_go")
            pe.reg_mov(pass_no, 0)
            pe.reg_mov(go_on, 1)

            def input_part(t, tau_par, b):
                g = gates[b][tau_par]
                nc.tensor.matmul(g[:, 0:4 * HS], bias_w[:, :], bias_cols, start=True, stop=False, skip_group_check=True)
                for q in (3, 0, 1, 2):
                    nc.tensor.matmul(g[:, q * HS:(q + 1) * HS], W("w_ih", q * D, (q + 1) * D),
                                     xls[:, b * (NC // 2):(b + 1) * (NC // 2), bass.ds(t * SPC, SPC)],
                                     start=False, stop=False, skip_group_check=True)

            def hidden_part(t, tau_par, b, done):
                g = gates[b][tau_par]
                wait(pe, hid_ready, done)
                for q in (3, 0, 1, 2):
                    last = nc.tensor.matmul(g[:, q * HS:(q + 1) * HS], W("w_hh", q * D, (q + 1) * D),
                                            hs[:, t, b * HS:(b + 1) * HS],
                                            start=False, stop=(q == 2), skip_group_check=True)
                last.then_inc(gates_ready, 1)

            def two_steps(t, pn, done, first, last_pair):
                for e in range(2):
                    for b in range(2):
                        hidden_part(t + e, e, b, 0 if first and e == 0 else done + 2 * (t + e) + (b - 1))
                        if not (last_pair and e == 1):
                            input_part(t + e + 1, 1 - e, b)

            def run_steps(begin, pn, done):
                for b in range(2):
                    input_part(begin, 0, b)
                two_steps(begin, pn, done, True, False)
                with pe.Fori(begin + 2, SEG - 3, 2) as t:
                    two_steps(t, pn, done, False, False)
                two_steps(SEG - 2, pn, done, False, True)

            run_steps(SEG - WARM, 0, -2 * (SEG - WARM))
            pe.wait_ge(guess_ready, 1)
            with pe.While(lambda: pe.snap(go_on)):
                pn = pe.snap(pass_no)
                run_steps(0, pn, 2 * SEG * pn + 2 * WARM)
                pe.wait_ge(agree_ready, pn + 1)
                nc.tensor.matmul(count_ps[:, 0:1], ones_w[:, :], agree, start=True, stop=True).then_inc(agree_sum, 1)
                pe.wait_ge(flag_ready, pn + 1)
                pe.sem_inc(flag_seen, 1)
                pe.reg_load(go_on, flag[0:1, 0:1])
                pe.reg_add(pass_no, pass_no, 1)

            pe.wait_ge(lstm_init, 3)
            def chunk(i, q):
                for l, ready, used in ((0, l0_ready, l0b_ready), (1, l1_ready, gsel_ready)):
                    wait(pe, used, i - 1)
                    nc.tensor.matmul(l_bank[l][q][:, :], wlin[:, l * P:(l + 1) * P],
                                     hs[:, 1:SEG + 1, bass.ds(i * SPC, SPC)],
                                     start=True, stop=True).then_inc(ready, 1)

            by_chunk(pe, chunk)

        @block.scalar
        def _(act):
            act.dma_start(bias_in[0:4, :], lstm_bias).then_inc(bias_loaded, 16)
            act.dma_start(bias_in[32:36, :], lstm_bias).then_inc(bias_loaded, 16)
            act.dma_start(bias_in[64:68, :], lstm_bias).then_inc(bias_loaded, 16)
            act.preload_act_table_set(LN_EXP)
            act.wait_ge(consts_ready, 1)
            for g in range(4):
                act.wait_ge(row_centred, g + 1)
                if g:
                    act.wait_ge(row_var, g)
                nc.scalar.activation(sq_rows, xn[:, 16 * g:16 * g + 16, :], ACT.Square).then_inc(row_sq, 1)
                act.wait_ge(row_var, g + 1)
                nc.scalar.activation(stat[:, 2, 16 * g:16 * g + 16], stat[:, 1, 16 * g:16 * g + 16], ACT.Ln,
                                     bias=eps[:, :], scale=1.0 / D).then_inc(row_ln, 1)
                act.wait_ge(row_ln, g + 1)
                nc.scalar.activation(stat[:, 3, 16 * g:16 * g + 16], stat[:, 2, 16 * g:16 * g + 16], ACT.Exp,
                                     scale=-0.5).then_inc(row_rstd, 1)
            act.wait_ge(consts_in, 32)
            o = VOFF["a_log"]
            nc.scalar.activation(a_neg[:, :], v_sb[:, o:o + HV * DS], ACT.Exp).then_inc(init_done, 1)

            def step(k, par, adj, pre, scan, post):
                cs, q = k - 2, 1 - par

                def written(name):
                    act.wait_ge(shared_written, shared_index(name, k, pre, post) + 1)

                def pre_part(s):
                    if s == 0:
                        written("gcn")
                        nc.scalar.activation(ht, shared[:, :], ACT.Relu, bias=V("gcn_b")).then_inc(shared_read, 1)
                    if s == 1:
                        act.wait_ge(shared_read, shared_index("mean", k, pre, post) + 1)
                        nc.scalar.activation(sq, ht, ACT.Square).then_inc(squared, 1)
                    if s == 2:
                        written("var")
                        nc.scalar.activation(rs, shared[:, :], ACT.Ln, bias=eps[:, :]).then_inc(shared_read, 1)
                        act.wait_ge(shared_read, shared_index("var", k, pre, post) + 1)
                        nc.scalar.activation(rs, rs, ACT.Exp, scale=-0.5).then_inc(rstd_ready, 1)
                    if s == 3:
                        act.wait_ge(hn_ready, k)
                        nc.scalar.activation(ht, ht, ACT.Identity, bias=V("ln_b"), scale=V("ln_g")).then_inc(h_ready, 1)
                    if s == 5:
                        for h in range(HV):
                            written(f"xc{h}")
                            nc.scalar.activation(xc[q][:, h, HALO:HALO + CH], shared[:, :], ACT.Copy).then_inc(shared_read, 1)
                        act.wait_ge(shared_read, shared_index("xc1", k, pre, post) + 1)
                        act.wait_ge(halo_ready, k)
                        for h in range(HV):
                            last = nc.scalar.activation(wd[:, h, :], xc[q][:, h, 0:CH], ACT.Identity,
                                                        bias=V("conv_b", h), scale=V("conv_w", h * TAPS))
                        last.then_inc(tap_ready, 1)
                        nc.scalar.activation(xc[1 - q][:, :, 0:HALO], xc[q][:, :, CH:CH + HALO], ACT.Copy).then_inc(halo_ready, 1)
                    if s == 6:
                        for h in range(HV):
                            written(f"z{h}")
                            nc.scalar.activation(sz[q][:, h, :], shared[:, :], ACT.Copy).then_inc(shared_read, 1)
                    if s == 8:
                        act.wait_ge(tap_done, HALO * k)
                        nc.scalar.activation(u[q], wd, ACT.Silu).then_inc(u_ready, 1)
                        act.wait_ge(shared_read, shared_index("z1", k, pre, post) + 1)
                        nc.scalar.activation(sz[q], sz[q], ACT.Silu).then_inc(sz_ready, 1)
                        act.preload_act_table_set(LN_EXP)
                    if s == 9:
                        written("dbc")
                        nc.scalar.activation(dbc[0:XPW, :], shared[0:XPW, :], ACT.Copy).then_inc(shared_read, 1)
                        act.wait_ge(shared_read, shared_index("dbc", k, pre, post) + 1)
                        nc.scalar.activation(bc_parts[q][:, :], dbc[0:PARTS * BC, :], ACT.Copy).then_inc(high_ready, 1)
                    if s == 10:
                        for h in range(HV):
                            written(f"dt{h}")
                            nc.scalar.activation(wa[:, h, :], shared[:, :], ACT.Relu, bias=V("b_dt", h)).then_inc(pos_dt, 1)
                            nc.scalar.activation(wb[:, h, :], shared[:, :], ACT.Abs, bias=V("b_dt", h)).then_inc(shared_read, 1)
                    if s == 11:
                        act.wait_ge(shared_read, shared_index("dt1", k, pre, post) + 1)
                        nc.scalar.activation(wb, wb, ACT.Exp, scale=-1.0).then_inc(exp_dt, 1)
                        act.wait_ge(exp_dt, k)
                        nc.scalar.activation(wc, wb, ACT.Identity, bias=1.0).then_inc(one_dt, 1)
                        act.wait_ge(one_dt, k)
                        nc.scalar.activation(wd, wc, ACT.Ln).then_inc(log_dt, 1)
                    if s == 12:
                        act.wait_ge(r1_ready, k)
                        nc.scalar.activation(bc_mid[:, :], r1[0:PARTS * BC, :], ACT.Copy).then_inc(mid_rounded, 1)
                        act.wait_ge(mid_rounded, k)
                        nc.scalar.activation(bc_parts[q][BC:2 * BC, :], bc_mid[BC:2 * BC, :], ACT.Copy).then_inc(mid_ready, 1)

                def post_part(s):
                    if s == 0:
                        for h in range(HV):
                            last = nc.scalar.activation(yv[:, h, :], u[q][:, h, :], ACT.Copy, scale=V("d_skip", h))
                        last.then_inc(skip_ready, 1)
                    if s == 4:
                        act.wait_ge(shared_read, shared_index("out", k, pre, post) + 1)
                        act.dma_start(x1_dram[k - 3], x1c).then_inc(x1_stored, 16)
                    if s == 5:
                        act.wait_ge(shared_read, shared_index("pmean", k, pre, post) + 1)
                        nc.scalar.activation(psq, xd, ACT.Square).then_inc(psq_ready, 1)
                    if s == 7:
                        written("pvar")
                        nc.scalar.activation(prs, shared[:, :], ACT.Ln, bias=eps[:, :]).then_inc(shared_read, 1)
                        act.wait_ge(shared_read, shared_index("pvar", k, pre, post) + 1)
                        nc.scalar.activation(prs, prs, ACT.Exp, scale=-0.5).then_inc(prstd_ready, 1)
                    if s == 12:
                        act.wait_ge(xl_ready, k - 2)
                        act.dma_start(xl_dram[k - 3], xlc).then_inc(xl_stored, 16)

                for s in range(16):
                    if pre and s == 0:
                        act.wait_ge(adj_used, PIECES * k)
                        nc.scalar.activation(m1, mixed[:, :], ACT.Copy).then_inc(mixed_copied, 1)
                    if scan:
                        if s == 0:
                            act.wait_ge(dt_ready, cs + 1)
                        for h in range(HV):
                            wait(act, scan_done, HV * DS * cs + (HV * (s - 1) + h + 1))
                            nc.scalar.activation(da[h][:, :], dt[par][:, h, :], ACT.Exp,
                                                 scale=a_neg[:, h * DS + s:h * DS + s + 1]).then_inc(da_ready, 1)
                    if pre:
                        pre_part(s)
                    if post:
                        post_part(s)

            iterations(act, step)

            act.wait_ge(lstm_init, 2)
            act.preload_act_table_set("sigmoid_and_others")
            pass_no = act.alloc_register("act_pass")
            go_on = act.alloc_register("act_go")
            act.reg_mov(pass_no, 0)
            act.reg_mov(go_on, 1)
            def run_steps(begin, base):
                with act.Fori(begin, SEG - 1, 2) as t:
                    for e in range(2):
                        for b in range(2):
                            done = base + 2 * t + (2 * e + b + 1)
                            g = gates[b][e]
                            act.wait_ge(gates_ready, done)
                            nc.scalar.activation(tg[b], g[:, 3 * HS:4 * HS], ACT.Tanh).then_inc(tg_ready, 1)
                            nc.scalar.activation(sg[b], g[:, 0:3 * HS], ACT.Sigmoid).then_inc(sg_ready, 1)
                            act.wait_ge(cell_ready, done)
                            nc.scalar.activation(tc[b], c_st[:, b * HS:(b + 1) * HS], ACT.Tanh).then_inc(tc_ready, 1)

            run_steps(SEG - WARM, -2 * (SEG - WARM))
            with act.While(lambda: act.snap(go_on)):
                pn = act.snap(pass_no)
                run_steps(0, 2 * SEG * pn + 2 * WARM)
                act.wait_ge(flag_ready, pn + 1)
                act.sem_inc(flag_seen, 1)
                act.reg_load(go_on, flag[0:1, 0:1])
                act.reg_add(pass_no, pass_no, 1)

            def chunk(i, q):
                act.wait_ge(l0_ready, i + 1)
                wait(act, gsel_ready, i - 1)
                nc.scalar.activation(l0b[q], l_bank[0][q][:, :], ACT.Identity, bias=V("b_lin", 0)).then_inc(l0b_ready, 1)
                wait(act, dbl_ready, i - 1)
                nc.scalar.activation(h2[q].rearrange("p (s t) -> p t s", s=SPC),
                                     hs[:, 1:SEG + 1, bass.ds(i * SPC, SPC)], ACT.Copy, scale=2.0).then_inc(h2_ready, 1)

            by_chunk(act, chunk)

        @block.gpsimd
        def _(pool):
            nc.gpsimd.memset(sel[:, :], 0.0).then_inc(sel_ready, 1)
            view = sel[:, :].rearrange("p (n m) -> p n m", m=P)
            for g in range(PARTS):
                pool.wait_ge(sel_ready, g + 1)
                nc.gpsimd.affine_select(out=view, in_=view, compare_op=ALU.not_equal, fill=1.0, base=-BC * g,
                                        pattern=[[-1, BC], [0, P]], channel_multiplier=1).then_inc(sel_ready, 1)
            pool.wait_ge(consts_in, 32)

            def step(k, par, adj, pre, scan, post):
                cs, q = k - 2, 1 - par

                def pre_part(s):
                    if s == 12:
                        pool.wait_ge(log_dt, k)
                        pool.wait_ge(rem_dt, k)
                        nc.gpsimd.tensor_tensor(out=wb, in0=wd, in1=wb, op=ALU.subtract).then_inc(sum_dt, 1)
                    if s == 13:
                        pool.wait_ge(sum_dt, k)
                        pool.wait_ge(pos_dt, HV * k)
                        nc.gpsimd.tensor_tensor(out=dt[q], in0=wa, in1=wb, op=ALU.add).then_inc(dt_ready, 1)
                    if s == 14:
                        pool.wait_ge(dt_ready, k)
                        nc.gpsimd.tensor_tensor(out=dtu[q], in0=dt[q], in1=u[q], op=ALU.mult).then_inc(dtu_ready, 1)

                def post_part(s):
                    if s == 0:
                        pool.wait_ge(y_added, (DS - 1) * (k - 2))
                        pool.wait_ge(skip_ready, k - 2)
                        nc.gpsimd.tensor_tensor(out=yv, in0=yv, in1=acc, op=ALU.add).then_inc(y_skip, 1)
                        pool.wait_ge(y_skip, k - 2)
                        nc.gpsimd.tensor_tensor(out=yv, in0=yv, in1=sz[q], op=ALU.mult).then_inc(y_ready, 1)
                    if s == 8:
                        pool.wait_ge(prstd_ready, k - 2)
                        wait(pool, xl_stored, 16 * (k - 3))
                        nc.gpsimd.tensor_tensor(out=xlc.rearrange("p (t s) -> p s t", s=SPC),
                                                in0=xd.rearrange("p (s t) -> p s t", s=SPC),
                                                in1=prs.rearrange("p (s t) -> p s t", s=SPC),
                                                op=ALU.mult).then_inc(xl_ready, 1)

                def add(n):
                    pool.wait_ge(hc_done, DS * cs + n + 1)
                    if n > 1:
                        pool.wait_ge(y_added, (DS - 1) * cs + (n - 1))
                    nc.gpsimd.tensor_tensor(out=acc, in0=hc[0] if n == 1 else acc, in1=hc[n % 2],
                                            op=ALU.add).then_inc(y_added, 1)

                for s in range(16):
                    if post and s == 0:
                        post_part(s)
                    if scan and s >= 2:
                        add(s - 1)
                    if pre:
                        pre_part(s)
                    if post and s > 0:
                        post_part(s)
                if scan:
                    add(DS - 1)

            iterations(pool, step)

            pool.wait_ge(lstm_init, 3)
            def chunk(i, q):
                pool.wait_ge(x1f_in[q], 8 * (i - q) + 16)
                pool.wait_ge(h2_ready, i + 1)
                nc.gpsimd.tensor_tensor(out=fin_all[:, bass.ds(i * CH, CH)], in0=h2[q], in1=x1f[q], op=ALU.add).then_inc(dbl_ready, 1)
                pool.wait_ge(inc_ready, i + 1)
                wait(pool, fwd_done, i - 1)
                nc.gpsimd.tensor_tensor(out=prefix[q], in0=inc_all[:, bass.ds(i * CH, CH)], in1=wsel[q],
                                        op=ALU.subtract).then_inc(pre_ready, 1)

            by_chunk(pool, chunk)

        @block.vector
        def _(dve):
            nc.vector.memset(mean_w[:, :], 1.0 / D)
            nc.vector.memset(eps[:, :], EPS)
            nc.vector.memset(hstate[:, :], 0.0)
            nc.vector.memset(xc[0][:, :, 0:HALO], 0.0).then_inc(halo_ready, 1)
            nc.vector.memset(ones_w[:, :], 1.0).then_inc(consts_ready, 1)
            for g in range(4):
                dve.wait_ge(x_in[g], 16)
                blk = slice(16 * g, 16 * g + 16)
                xg = xn[:, blk, :]

                def spread(k):
                    return stat[:, k, blk].unsqueeze(2).broadcast_to([P, 16, D])

                nc.vector.reduce_sum(stat[:, 0, blk], xg, axis=AX.X).then_inc(row_sum, 1)
                dve.wait_ge(row_sum, g + 1)
                nc.vector.tensor_scalar(stat[:, 0, blk], stat[:, 0, blk], 1.0 / D, None, ALU.mult).then_inc(row_mean, 1)
                dve.wait_ge(row_mean, g + 1)
                nc.vector.tensor_tensor(out=xg, in0=xg, in1=spread(0), op=ALU.subtract).then_inc(row_centred, 1)
                dve.wait_ge(row_sq, g + 1)
                nc.vector.reduce_sum(stat[:, 1, blk], sq_rows, axis=AX.X).then_inc(row_var, 1)
                dve.wait_ge(row_rstd, g + 1)
                nc.vector.tensor_tensor(out=xg, in0=xg, in1=spread(3), op=ALU.mult).then_inc(xn_ready, 1)
            dve.wait_ge(init_done, 1)
            nc.vector.tensor_scalar(a_neg[:, :], a_neg[:, :], -1.0, None, ALU.mult).then_inc(init_done, 1)
            nc.vector.tensor_scalar(negbw[:, :], V("bw"), -1.0, None, ALU.mult)
            nc.vector.memset(bias_w[:, :], 0.0).then_inc(bias_ready, 1)
            dve.wait_ge(bias_loaded, 48)
            n = [0]

            def link(ins):
                n[0] += 1
                ins.then_inc(check_step, 1)
                dve.wait_ge(check_step, n[0])

            full, tail = bias_in[:, 0:P], bias_in[:, P:2 * P]
            for i in range(PARTS):
                r = slice(32 * i, 32 * i + 4)
                link(nc.vector.tensor_tensor(out=full[r], in0=full[r], in1=tail[r], op=ALU.add))
                link(nc.vector.tensor_copy(bias_mid[r, :], full[r]))
                for _ in range(i):
                    link(nc.vector.tensor_tensor(out=full[r], in0=full[r], in1=bias_mid[r, :], op=ALU.subtract))
                    link(nc.vector.tensor_copy(bias_mid[r, :], full[r]))
                if i == 0:
                    dve.wait_ge(bias_ready, 1)
                link(nc.vector.tensor_copy(bias_w[r, :], bias_mid[r, :]))
            dve.sem_inc(bias_ready, 1)

            def step(k, par, adj, pre, scan, post):
                cs, q = k - 2, 1 - par

                def written(name):
                    dve.wait_ge(shared_written, shared_index(name, k, pre, post) + 1)

                def side_part(s):
                    if pre and s == 1:
                        written("mean")
                        nc.vector.tensor_tensor(out=ht, in0=ht, in1=shared[:, :], op=ALU.subtract).then_inc(shared_read, 1)
                    if post and s == 3:
                        written("out")
                        dve.wait_ge(xt_in[q], 8 * (k - 3 - q) + 16)
                        wait(dve, x1_stored, 16 * (k - 3))
                        nc.vector.tensor_tensor(out=x1c, in0=xt[q], in1=shared[:, :], op=ALU.add).then_inc(shared_read, 1)
                    if pre and s == 3:
                        dve.wait_ge(rstd_ready, k)
                        nc.vector.tensor_tensor(out=ht, in0=ht, in1=rs, op=ALU.mult).then_inc(hn_ready, 1)
                    if post and s == 4:
                        written("pmean")
                        nc.vector.tensor_tensor(out=xd, in0=x1c, in1=shared[:, :], op=ALU.subtract).then_inc(shared_read, 1)
                    if pre and s in (6, 7):
                        for i in ((1,) if s == 6 else (2, 3)):
                            if i == 1:
                                dve.wait_ge(tap_ready, k)
                            else:
                                dve.wait_ge(tap_done, HALO * (k - 1) + (i - 1))
                            for h in range(HV):
                                last = nc.vector.scalar_tensor_tensor(
                                    out=wd[:, h, :], in0=xc[q][:, h, i:i + CH], scalar=V("conv_w", h * TAPS + i),
                                    in1=wd[:, h, :], op0=ALU.mult, op1=ALU.add)
                            last.then_inc(tap_done, 1)
                    if pre and s == 10:
                        dve.wait_ge(high_ready, k)
                        nc.vector.tensor_tensor(out=r1[0:PARTS * BC, :], in0=dbc[0:PARTS * BC, :], in1=bc_parts[q][:, :],
                                                op=ALU.subtract).then_inc(r1_ready, 1)
                    if pre and s == 12:
                        dve.wait_ge(one_dt, k)
                        nc.vector.scalar_tensor_tensor(out=wb, in0=wc, scalar=-1.0, in1=wb, op0=ALU.add,
                                                       op1=ALU.subtract).then_inc(rem_dt, 1)
                    if pre and s == 13:
                        dve.wait_ge(mid_rounded, k)
                        nc.vector.tensor_tensor(out=bc_parts[q][2 * BC:3 * BC, :], in0=r1[2 * BC:3 * BC, :],
                                                in1=bc_mid[2 * BC:3 * BC, :], op=ALU.subtract).then_inc(low_ready, 1)

                def both(ap):
                    return ap[:, :].unsqueeze(1).broadcast_to([P, HV, CH])

                def make_dbu(n):
                    dve.wait_ge(b_ready, DS * cs + n + 1)
                    wait(dve, scan_done, HV * (DS * cs + n - 1) if isinstance(cs, int) else HV * DS * cs + HV * (n - 1))
                    nc.vector.tensor_tensor(out=dbu[n % 2], in0=dtu[par], in1=both(b_bank[n % 2]),
                                            op=ALU.mult).then_inc(dbu_done, 1)

                def make_hc(n):
                    dve.wait_ge(c_ready, DS * cs + n + 1)
                    dve.wait_ge(scan_done, HV * DS * cs + HV * (n + 1))
                    wait(dve, y_added, (DS - 1) * cs + (max(n - 2, 1) if n >= 2 else n - 1))
                    nc.vector.tensor_tensor(out=hc[n % 2], in0=hb[n % 2], in1=both(c_bank[n % 2]),
                                            op=ALU.mult).then_inc(hc_done, 1)
                    nc.vector.tensor_copy(hstate[:, HV * n:HV * n + HV], hb[n % 2][:, :, CH - 1]).then_inc(state_saved, 1)

                for s in range(16):
                    side_part(s)
                    if not scan:
                        continue
                    if s == 0:
                        dve.wait_ge(dtu_ready, cs + 1)
                        make_dbu(0)
                    if s < DS - 1:
                        make_dbu(s + 1)
                    for h in range(HV):
                        dve.wait_ge(da_ready, HV * DS * cs + (HV * s + h + 1))
                        if h == 0:
                            dve.wait_ge(dbu_done, DS * cs + s + 1)
                            wait(dve, state_saved, DS * cs + (s - 1))
                            wait(dve, hc_done, DS * cs + (s - 1))
                        nc.vector.tensor_tensor_scan(hb[s % 2][:, h, :], da[h][:, :], dbu[s % 2][:, h, :],
                                                     hstate[:, HV * s + h:HV * s + h + 1],
                                                     ALU.mult, ALU.add).then_inc(scan_done, 1)
                    if s >= 1:
                        make_hc(s - 1)
                if scan:
                    make_hc(DS - 1)

            iterations(dve, step)

            dve.wait_ge(x1_stored, 16 * NC)
            dve.wait_ge(xl_stored, 16 * NC)
            dve.wait_ge(adj_used, PIECES * NC)
            nc.vector.memset(hs[:, 0, :], 0.0)
            if WARM < SEG:
                nc.vector.memset(hs[:, SEG - WARM, :], 0.0)
            nc.vector.memset(c_in, 0.0)
            nc.vector.memset(passes, 0.0)
            nc.vector.memset(run_total, 0.0)
            nc.vector.memset(c_st, 0.0).then_inc(lstm_init, 1)
            dve.wait_ge(lstm_init, 1)
            for l in range(2):
                last = nc.vector.tensor_copy(wlin[:, l * P:(l + 1) * P], V("w_lin", l).broadcast_to([P, P]))
            last.then_inc(lstm_init, 1)
            pass_no = dve.alloc_register("dve_pass")
            go_on = dve.alloc_register("dve_go")
            dve.reg_mov(pass_no, 0)
            dve.reg_mov(go_on, 1)
            checks = 8

            def run_steps(begin, base):
                with dve.Fori(begin, SEG) as t:
                    for b in range(2):
                        seg = slice(b * HS, (b + 1) * HS)
                        done = base + 2 * t + (b + 1)
                        dve.wait_ge(tg_ready, done)
                        dve.wait_ge(sg_ready, done)
                        nc.vector.tensor_tensor(out=fc[b], in0=sg[b][:, HS:2 * HS], in1=c_st[:, seg], op=ALU.mult).then_inc(fc_ready, 1)
                        nc.vector.tensor_tensor(out=ig[b], in0=sg[b][:, 0:HS], in1=tg[b], op=ALU.mult).then_inc(ig_ready, 1)
                        dve.wait_ge(fc_ready, done)
                        dve.wait_ge(ig_ready, done)
                        nc.vector.tensor_tensor(out=c_st[:, seg], in0=fc[b], in1=ig[b], op=ALU.add).then_inc(cell_ready, 1)
                        dve.wait_ge(tc_ready, done)
                        nc.vector.tensor_tensor(out=hs[:, t + 1, seg], in0=sg[b][:, 2 * HS:3 * HS], in1=tc[b],
                                                op=ALU.mult).then_inc(hid_ready, 1)

            run_steps(SEG - WARM, -2 * (SEG - WARM))
            dve.wait_ge(hid_ready, 2 * WARM)
            nc.vector.tensor_copy(hs[:, 0, 1:NSEG], hs[:, SEG, 0:NSEG - 1])
            link(nc.vector.tensor_copy(c_in[:, 1:NSEG], c_st[:, 0:NSEG - 1]))
            nc.vector.tensor_copy(c_st, c_in).then_inc(guess_ready, 1)
            dve.wait_ge(guess_ready, 1)
            links_before = n[0]
            with dve.While(lambda: dve.snap(go_on)):
                pn = dve.snap(pass_no)
                run_steps(0, 2 * SEG * pn + 2 * WARM)
                base = checks * pn + links_before
                k = [0]

                def then(ins):
                    k[0] += 1
                    ins.then_inc(check_step, 1)
                    dve.wait_ge(check_step, base + k[0])

                dve.wait_ge(hid_ready, 2 * SEG * pn + 2 * (WARM + SEG))
                E = NSEG - 1
                nc.vector.tensor_tensor(out=diff[:, 0:E], in0=hs[:, SEG, 0:E], in1=hs[:, 0, 1:NSEG], op=ALU.subtract)
                nc.vector.tensor_scalar(passes, passes, 1.0, None, ALU.add)
                then(nc.vector.tensor_tensor(out=diff[:, E:2 * E], in0=c_st[:, 0:E], in1=c_in[:, 1:NSEG], op=ALU.subtract))
                nc.vector.tensor_copy(hs[:, 0, 1:NSEG], hs[:, SEG, 0:E])
                nc.vector.tensor_copy(c_in[:, 1:NSEG], c_st[:, 0:E])
                then(nc.vector.tensor_tensor(out=diff, in0=diff, in1=diff, op=ALU.mult))
                then(nc.vector.tensor_scalar(diff, diff, TOL * TOL, None, ALU.is_le))
                then(nc.vector.tensor_scalar(alive, passes, float(NSEG), None, ALU.is_lt))
                nc.vector.reduce_sum(agree, diff, axis=AX.X).then_inc(agree_ready, 1)
                then(nc.vector.tensor_copy(c_st, c_in))
                dve.wait_ge(agree_sum, pn + 1)
                nc.vector.scalar_tensor_tensor(out=flag[:, :], in0=count_ps[0:1, 0:1], scalar=float(2 * E * P),
                                               in1=alive[0:1, :], op0=ALU.is_lt, op1=ALU.mult).then_inc(flag_ready, 1)
                dve.wait_ge(flag_ready, pn + 1)
                dve.sem_inc(flag_seen, 1)
                dve.reg_load(go_on, flag[0:1, 0:1])
                for _ in range(checks - k[0]):
                    dve.sem_inc(check_step, 1)
                dve.reg_add(pass_no, pass_no, 1)
            dve.sem_inc(lstm_init, 1)

            def add_prefix(i, q):
                t0 = i * CH
                dve.wait_ge(pre_ready, i + 1)
                dve.wait_ge(dbl_ready, i + 1)
                nc.vector.scalar_tensor_tensor(out=fin_all[:, bass.ds(t0, CH)], in0=prefix[q], scalar=V("fw"),
                                               in1=fin_all[:, bass.ds(t0, CH)], op0=ALU.mult, op1=ALU.add).then_inc(fwd_done, 1)

            def chunk(i, q):
                t0 = i * CH
                dve.wait_ge(l1_ready, i + 1)
                dve.wait_ge(l0b_ready, i + 1)
                wait(dve, wsel_ready, i - 1)
                nc.vector.scalar_tensor_tensor(out=gsel[q], in0=l_bank[1][q][:, :], scalar=V("b_lin", 1), in1=l0b[q],
                                               op0=ALU.add, op1=ALU.is_gt).then_inc(gsel_ready, 1)
                dve.wait_ge(gsel_ready, i + 1)
                wait(dve, pre_ready, i - 1)
                nc.vector.tensor_tensor(out=wsel[q].rearrange("p (s t) -> p t s", s=SPC),
                                        in0=gsel[q].rearrange("p (t s) -> p t s", s=SPC),
                                        in1=hs[:, 1:SEG + 1, bass.ds(i * SPC, SPC)], op=ALU.mult).then_inc(wsel_ready, 1)
                dve.wait_ge(wsel_ready, i + 1)
                wait(dve, total_ready, i)
                nc.vector.tensor_tensor_scan(inc_all[:, bass.ds(t0, CH)], wsel[q], wsel[q], run_total,
                                             ALU.add, ALU.bypass).then_inc(inc_ready, 1)
                dve.wait_ge(inc_ready, i + 1)
                nc.vector.tensor_copy(run_total, inc_all[:, bass.ds(t0 + (CH - 1), 1)]).then_inc(total_ready, 1)
                if not (isinstance(i, int) and i == 0):
                    add_prefix(i - 1, 1 - q)

            by_chunk(dve, chunk)
            add_prefix(NC - 1, 1)
            dve.wait_ge(total_ready, NC)
            dve.wait_ge(pre_ready, NC)
            def chunk(i, q):
                t0 = i * CH
                nc.vector.tensor_scalar(inc_all[:, bass.ds(t0, CH)], inc_all[:, bass.ds(t0, CH)], run_total, negbw[:, :],
                                        ALU.subtract, ALU.mult).then_inc(suf_ready, 1)
                dve.wait_ge(suf_ready, i + 1)
                wait(dve, out_done[q], 8 * (i - q))
                nc.vector.tensor_tensor(out=ob[q], in0=inc_all[:, bass.ds(t0, CH)], in1=fin_all[:, bass.ds(t0, CH)],
                                        op=ALU.add).then_inc(ob_ready, 1)

            by_chunk(dve, chunk)


_INS = ["adj_t", "x_rows", "x_t", "weights", "vectors", "lstm_bias"]


def kernel(**inputs):
    import concourse.bacc as bacc
    from concourse.bass_utils import run_bass_kernel_spmd

    a = {k: np.asarray(v) for k, v in inputs.items()}
    g, f = "L0_gnn_", "L0_ffn_"
    x, adj = a["x"], a["adj"]

    def gate_columns(w):
        w = w.T.reshape(D, 4, D)
        return np.concatenate([w[:, 0], w[:, 1], w[:, 3], w[:, 2]], axis=1)

    def by_half(v):
        v = v.reshape(HV, P, -1)
        return np.concatenate([v[h] for h in range(HV)], axis=1)

    w_xp = a[g + "w_xp"]
    w_xp = np.concatenate([w_xp[:, DR:]] * PARTS + [w_xp[:, :DR]], axis=1)
    w_dt = np.zeros((P, DI), np.float32)
    w_dt[PARTS * BC:XPW] = a[g + "w_dt"]
    weights = np.concatenate([a[g + "gcn_w"], a[g + "w_in"], by_half(w_xp), w_dt, by_half(a[g + "w_out"]),
                              gate_columns(a[f + "W_ih"]), gate_columns(a[f + "W_hh"])], axis=1)

    def col(v):
        return v.reshape(P, 1)

    vectors = np.concatenate([col(a[g + "gcn_b"]), col(a[g + "ln_g"]), col(a[g + "ln_b"]), by_half(a[g + "conv_b"]),
                              by_half(a[g + "conv_w"]), by_half(a[g + "b_dt"]), by_half(a[g + "D_skip"]),
                              col(a[f + "fw_att"]), col(a[f + "bw_att"]), by_half(a[g + "A_log"]),
                              a[f + "W_lin"].T, np.broadcast_to(a[f + "b_lin"], (P, 2))], axis=1)

    def gate_rows(b):
        b = b.reshape(4, D)
        return b[[0, 1, 3, 2]]

    arrays = dict(
        adj_t=adj.reshape(NC, CH, P, BLK).transpose(0, 2, 3, 1).reshape(NC, P, BLK * CH),
        x_rows=x.reshape(P, BLK * D),
        x_t=x.reshape(NC, CH, D).transpose(0, 2, 1),
        weights=weights, vectors=vectors,
        lstm_bias=np.concatenate([gate_rows(a[f + "b_ih"]), gate_rows(a[f + "b_hh"])], axis=1),
    )
    arrays = {k: np.ascontiguousarray(v) for k, v in arrays.items()}
    nc = bacc.Bacc("TRN2", target_bir_lowering=False, num_devices=1)
    args = [nc.dram_tensor(n, arrays[n].shape, mybir.dt.from_np(arrays[n].dtype), kind="ExternalInput").ap() for n in _INS]
    out = nc.dram_tensor("out_t", (NC, P, CH), mybir.dt.float32, kind="ExternalOutput").ap()
    build(nc, *args, out)
    r = run_bass_kernel_spmd(nc, [arrays], core_ids=[0])
    return np.ascontiguousarray(r.results[0]["out_t"].transpose(0, 2, 1).reshape(N, D))
```

```python
from contextlib import ExitStack

import numpy as np

import concourse.bass as bass
from concourse import mybir

N = 8192
D = 128
P = 128
CH = 512
NC = N // CH
BLK = N // P
PB = 4
PIECES = BLK // PB
RING = 4
XG = 16
GB = BLK // XG
DIRECT = NC - 3
DI = 256
HV = DI // P
DS = 16
TAPS = 4
HALO = TAPS - 1
DR = 8
BC = 2 * DS
XPW = 3 * BC + DR
SEG = 32
WARM = 32
NSEG = N // SEG
SPC = CH // SEG
HS = NSEG // 2
BG = 2
EPS = 1e-5
TOL = 2.0 ** -21
LN_EXP = "natural_log_exp_and_others"
PARTS = 3

WSIZE = dict(gcn=D, w_in=2 * DI, w_xp=HV * XPW, w_dt=DI, w_out=HV * D, w_ih=4 * D, w_hh=4 * D)
WOFF, _o = {}, 0
for _n, _s in WSIZE.items():
    WOFF[_n] = _o
    _o += _s
WTOT = _o
VSIZE = dict(gcn_b=1, ln_g=1, ln_b=1, conv_b=HV, conv_w=HV * TAPS, b_dt=HV, d_skip=HV, fw=1, bw=1,
             a_log=HV * DS, w_lin=2, b_lin=2, go_ih=2, go_hh=2)
VOFF, _o = {}, 0
for _n, _s in VSIZE.items():
    VOFF[_n] = _o
    _o += _s
VTOT = _o

SHARED = [("gcn", 0, "pre"), ("mean", 1, "pre"), ("var", 2, "pre"), ("out", 3, "post"),
          ("pmean", 4, "post"), ("xc0", 5, "pre"), ("xc1", 5.5, "pre"), ("z0", 6, "pre"),
          ("z1", 6.5, "pre"), ("pvar", 7, "post"), ("dbc", 9, "pre"), ("dt0", 10, "pre"),
          ("dt1", 10.5, "pre")]
PRE_STEPS = sum(s[2] == "pre" for s in SHARED)
POST_STEPS = sum(s[2] == "post" for s in SHARED)


def shared_index(step, k, pre, post):
    if isinstance(k, int):
        before = PRE_STEPS * (min(k, NC + 1) - 1) + POST_STEPS * max(0, k - 3)
    else:
        before = (PRE_STEPS + POST_STEPS) * k - (PRE_STEPS + 3 * POST_STEPS)
    names = [s[0] for s in SHARED if (pre and s[2] == "pre") or (post and s[2] == "post")]
    return before + names.index(step)


def drains(k):
    return isinstance(k, int) and k >= NC


def planned(k, s, stage):
    late = dict(pre=8, post=3)[stage]
    if not drains(k) or s < late:
        return s
    return None if s == late else s - 1


def wait(eng, sem, value):
    if not (isinstance(value, int) and value <= 0):
        eng.wait_ge(sem, value)


def build(nc, adj_t, x_rows, x_t, weights, vectors, lstm_bias, out_t):
    F32, BF, I32 = mybir.dt.float32, mybir.dt.bfloat16, mybir.dt.int32
    ALU, ACT, AX = mybir.AluOpType, mybir.ActivationFunctionType, mybir.AxisListType

    x1_dram = nc.dram_tensor("x1_scratch", (NC, P, CH), F32, kind="Internal").ap()
    xl_dram = nc.dram_tensor("xl_scratch", (NC, P, CH), F32, kind="Internal").ap()

    ctx = ExitStack()
    with ctx:
        def sb(name, shape, dt=F32):
            return ctx.enter_context(nc.sbuf_tensor(name, shape, dt))

        def sem(name):
            return ctx.enter_context(nc.semaphore(name))

        xh = sb("xh", [P, (SEG + 1) * NSEG])
        xn = xh[:, 0:N].rearrange("p (b d) -> p b d", d=D)
        hs = xh[:, :].rearrange("p (t s) -> p t s", s=NSEG)
        ring = sb("ring", [P, RING * PB * CH])
        xls = ring[:, :].rearrange("p (c t) -> p c t", c=NC)
        w_sb = sb("w_sb", [P, WTOT])
        v_sb = sb("v_sb", [P, VTOT])
        sel = sb("sel", [PARTS * BC, BC * P], BF)
        mean_w = sb("mean_w", [P, P])
        ones_w = sb("ones_w", [P, P])
        eps = sb("eps", [P, 1])
        a_neg = sb("a_neg", [P, HV * DS])
        negbw = sb("negbw", [P, 1])
        go_bias = sb("go_bias", [P, 2])
        bc_parts = [sb(f"bc_parts{i}", [PARTS * BC, CH], BF) for i in range(2)]
        bc_mid = sb("bc_mid", [PARTS * BC, CH], BF)
        hstate = sb("hstate", [P, DS * HV])
        bias_in = sb("bias_in", [PARTS * BC, 2 * P])
        bias_mid = sb("bias_mid", [PARTS * BC, P], BF)
        bias_w = sb("bias_w", [PARTS * BC, P], BF)
        flag = sb("flag", [1, 1], I32)

        WORK = 29 * 1024 + 512
        work = sb("work", [P, WORK])
        at = [0]

        def carve(n):
            a = at[0]
            at[0] += n
            assert at[0] <= WORK, at[0]
            return work[:, a:a + n]

        def halves(ap):
            return ap.rearrange("p (h t) -> p h t", h=HV)

        W2 = HV * CH
        dbu = [halves(carve(W2)) for _ in range(2)]
        hb = [halves(carve(W2)) for _ in range(2)]
        hc = [halves(carve(W2)) for _ in range(2)]
        xc = [halves(carve(HV * (HALO + CH + 1))) for _ in range(2)]
        u = [halves(carve(W2)) for _ in range(2)]
        sz = [halves(carve(W2)) for _ in range(2)]
        dt = [halves(carve(W2)) for _ in range(2)]
        dtu = [halves(carve(W2)) for _ in range(2)]
        acc = halves(carve(W2))
        yv = halves(carve(W2))
        pre_only = at[0]
        wa, wb, wc, wd = (halves(carve(W2)) for _ in range(4))
        m1, ht, sq, rs = (carve(CH) for _ in range(4))
        dbc, r1 = carve(CH), carve(CH)
        xt = [carve(CH) for _ in range(2)]
        x1c, xd, psq, prs = (carve(CH) for _ in range(4))
        xlc = carve(CH)
        sq_rows = work[:, 0:GB * D].rearrange("p (b d) -> p b d", d=D)
        stat = work[:, 4096:4096 + 4 * BLK].rearrange("p (k b) -> p k b", k=4)
        at[0] = 0
        x1_all = carve(N)
        inc = [carve(1 + CH) for _ in range(2)]
        wsel = [carve(CH) for _ in range(2)]
        h2 = [carve(CH) for _ in range(2)]
        inc_bw = [carve(CH) for _ in range(2)]
        at[0] = pre_only
        c_in = carve(NSEG)
        tg_c = carve(2 * NSEG)
        tg_c_half = tg_c.rearrange("p (k b s) -> p b k s", k=2, b=2)
        c_st = tg_c[:, NSEG:2 * NSEG]
        sg = [carve(3 * HS) for _ in range(2)]
        ig_fc = [carve(2 * HS) for _ in range(2)]
        tc = [carve(HS) for _ in range(2)]
        diff = carve(2 * (NSEG - 1))
        c_tol = carve(NSEG - 1)
        agree = carve(1)
        alive = carve(1)
        passes = carve(1)
        wlin = carve(P)
        tie = carve(1)
        bw_total = carve(1)

        fin_all = ring[:, 0:N]
        bias_cols = sel[:, :].rearrange("p (n m) -> p n m", m=P)[:, 0:BG, 0:HS]

        def W(name, lo=0, hi=None):
            o = WOFF[name]
            return w_sb[:, o + lo:o + (WSIZE[name] if hi is None else hi)]

        def V(name, i=0):
            return v_sb[:, VOFF[name] + i:VOFF[name] + i + 1]

        bank = [ctx.enter_context(nc.psum_tensor(f"bank{i}", [P, CH], F32)) for i in range(8)]
        mixed, shared = bank[0], bank[2]
        da = [bank[1][:, :], bank[7][:, :]]
        da_drain = [[xh[:, (4 + HV * i + h) * CH:(5 + HV * i + h) * CH] for h in range(HV)] for i in range(2)]
        y_bank = [bank[0], bank[7]]
        ident = xh[:, CH:CH + P]
        c_sb = [xh[:, (2 + i) * CH:(3 + i) * CH] for i in range(2)]
        b_bank = [bank[3], bank[4]]
        c_bank = [bank[5], bank[6]]
        gates = [[bank[0], bank[1]], [bank[2], bank[3]]]
        count_ps = bank[4]
        l_bank = [bank[5], bank[6]]

        def sems(names):
            return [sem(n) for n in names.split()]

        consts_in, bias_loaded = sems("consts_in bias_loaded")
        consts_ready, sel_ready, init_done, bias_ready = sems("consts_ready sel_ready init_done bias_ready")
        x_in = [sem(f"x_in{i}") for i in range(XG)]
        adj_in = [sem(f"adj_in{i}") for i in range(RING)]
        xt_in = [sem(f"xt_in{i}") for i in range(2)]
        row_sum, row_mean, row_centred, row_sq = sems("row_sum row_mean row_centred row_sq")
        row_var, row_ln, row_rstd, xn_ready = sems("row_var row_ln row_rstd xn_ready")
        adj_used, mixed_copied = sems("adj_used mixed_copied")
        shared_written, shared_read = sems("shared_written shared_read")
        squared, rstd_ready, hn_ready, h_ready = sems("squared rstd_ready hn_ready h_ready")
        halo_ready, tap_ready, tap_done, u_ready, sz_ready = sems("halo_ready tap_ready tap_done u_ready sz_ready")
        high_ready, r1_ready, mid_rounded, mid_ready, low_ready = sems("high_ready r1_ready mid_rounded mid_ready low_ready")
        pos_dt, exp_dt, one_dt, log_dt = sems("pos_dt exp_dt one_dt log_dt")
        rem_dt, sum_dt, dt_ready, dtu_ready = sems("rem_dt sum_dt dt_ready dtu_ready")
        b_ready, c_ready, da_ready, dbu_done = sems("b_ready c_ready da_ready dbu_done")
        scan_done, state_saved, hc_done, y_added = sems("scan_done state_saved hc_done y_added")
        c_copied, y_summed, ident_ready = sems("c_copied y_summed ident_ready")
        skip_ready, y_skip, y_ready = sems("skip_ready y_skip y_ready")
        x1_stored, psq_ready, prstd_ready = sems("x1_stored psq_ready prstd_ready")
        xl_ready, xl_stored, xls_in = sems("xl_ready xl_stored xls_in")
        lstm_init, guess_ready, gates_ready = sems("lstm_init guess_ready gates_ready")
        sg_ready, ig_fc_ready = sems("sg_ready ig_fc_ready")
        cell_ready, tc_ready, hid_ready = sems("cell_ready tc_ready hid_ready")
        agree_ready, agree_sum, flag_ready = sems("agree_ready agree_sum flag_ready")
        flag_seen, check_step = sems("flag_seen check_step")
        logit_ready, wsel_ready, inc_set, inc_ready = sems("logit_ready wsel_ready inc_set inc_ready")
        carry_ready, h2_ready, fwd_done, inc_bw_ready = sems("carry_ready h2_ready fwd_done inc_bw_ready")
        bwd_done, total_ready, x1_in, out_ready, out_done = sems("bwd_done total_ready x1_in out_ready out_done")

        block = ctx.enter_context(nc.Block())

        def iterations(eng, step):
            def flags(k):
                return k < NC, 1 <= k <= NC, 2 <= k <= NC + 1, 3 <= k <= NC + 2
            for k in range(4):
                step(k, k % 2, *flags(k))
            with eng.Fori(4, NC - 1, 2) as k:
                step(k, 0, True, True, True, True)
                step(k + 1, 1, True, True, True, True)
            for k in range(NC, NC + 3):
                step(k, k % 2, *flags(k))

        def by_chunk(eng, step):
            for c in range(2):
                step(c, c)
            with eng.Fori(2, NC - 1, 2) as c:
                step(c, 0)
                step(c + 1, 1)

        def make_xl(eng, ops, k):
            eng.wait_ge(prstd_ready, k - 2)
            if isinstance(k, int) and k - 3 >= DIRECT:
                dest = xls[:, k - 3, :]
                eng.wait_ge(adj_used, PIECES * NC)
            else:
                dest = xlc
                wait(eng, xl_stored, 16 * (k - 3))
            ops.tensor_tensor(out=dest.rearrange("p (t s) -> p s t", s=SPC), in0=xd.rearrange("p (s t) -> p s t", s=SPC),
                              in1=prs.rearrange("p (s t) -> p s t", s=SPC), op=ALU.mult).then_inc(xl_ready, 1)

        @block.sync
        def _(sp):
            def load_x(g):
                cols = slice(g * GB * D, (g + 1) * GB * D)
                sp.dma_start(xh[:, cols], x_rows[:, cols]).then_inc(x_in[g], 16)

            for g in range(2):
                load_x(g)

            def step(k, par, adj, pre, scan, post):
                if post:
                    wait(sp, x1_stored, 16 * (k - 4))
                    sp.dma_start(xt[1 - par], x_t[k - 3]).then_inc(xt_in[1 - par], 16)
                if adj:
                    for j in range(PIECES):
                        r = j % RING
                        wait(sp, adj_used, PIECES * k + (j - RING + 1))
                        sp.dma_start(ring[:, r * PB * CH:(r + 1) * PB * CH],
                                     adj_t[k, :, j * PB * CH:(j + 1) * PB * CH]).then_inc(adj_in[r], 16)
                        if isinstance(k, int) and k == 0:
                            if j + 2 < XG:
                                load_x(j + 2)
                            if j == PIECES - 1:
                                sp.dma_start(w_sb[:, :], weights).then_inc(consts_in, 16)
                                sp.dma_start(v_sb[:, :], vectors).then_inc(consts_in, 16)

            iterations(sp, step)
            sp.wait_ge(adj_used, PIECES * NC)
            sp.wait_ge(xl_stored, 16 * DIRECT)
            sp.dma_start(xls[:, 0:DIRECT, :], xl_dram[0:DIRECT].rearrange("c p t -> p c t")).then_inc(xls_in, 16)
            sp.wait_ge(x1_stored, 16 * NC)
            sp.wait_ge(xl_ready, NC)
            sp.dma_start(x1_all.rearrange("p (c t) -> p c t", c=NC), x1_dram.rearrange("c p t -> p c t")).then_inc(x1_in, 16)
            for i in range(NC):
                sp.wait_ge(out_ready, i + 1)
                sp.dma_start(out_t[i], fin_all[:, i * CH:(i + 1) * CH]).then_inc(out_done, 16)
            sp.wait_ge(out_done, 16 * NC)

        @block.tensor
        def _(pe):
            def step(k, par, adj, pre, scan, post):
                if isinstance(k, int) and k == 1:
                    pe.wait_ge(consts_in, 32)
                    pe.wait_ge(consts_ready, 1)
                    pe.wait_ge(sel_ready, 4)
                cs = k - 2

                def shared_step(name):
                    i = shared_index(name, k, pre, post)
                    wait(pe, shared_read, i)
                    out = shared[:, :]
                    if name == "gcn":
                        pe.wait_ge(mixed_copied, k)
                        ins = [(W("gcn"), m1)]
                    elif name == "mean":
                        ins = [(mean_w[:, :], ht)]
                    elif name == "var":
                        pe.wait_ge(squared, k)
                        ins = [(mean_w[:, :], sq)]
                    elif name in ("xc0", "xc1", "z0", "z1"):
                        b = ("xc0", "xc1", "z0", "z1").index(name)
                        pe.wait_ge(h_ready, k)
                        ins = [(W("w_in", b * P, (b + 1) * P), ht)]
                    elif name == "dbc":
                        pe.wait_ge(u_ready, k)
                        out = shared[0:XPW, :]
                        ins = [(W("w_xp", h * XPW, (h + 1) * XPW), u[1 - par][:, h, :]) for h in range(HV)]
                    elif name in ("dt0", "dt1"):
                        h = int(name[2])
                        o = WOFF["w_dt"] + h * P
                        ins = [(w_sb[0:XPW, o:o + P], dbc[0:XPW, :])]
                    elif name == "out":
                        pe.wait_ge(y_ready, k - 2)
                        ins = [(W("w_out", h * D, (h + 1) * D), yv[:, h, :]) for h in range(HV)]
                    elif name == "pmean":
                        ins = [(mean_w[:, :], x1c)]
                    else:
                        pe.wait_ge(psq_ready, k - 2)
                        ins = [(mean_w[:, :], psq)]
                    for n, (a, b) in enumerate(ins):
                        last = nc.tensor.matmul(out, a, b, start=(n == 0), stop=(n == len(ins) - 1))
                    last.then_inc(shared_written, 1)

                def spread(bank_, used, ready, row, n):
                    if used is not None:
                        wait(pe, used, DS * cs + (n - 1))
                    nc.tensor.matmul(bank_[n % 2][:, :], sel[:, row * P:(row + 1) * P],
                                     bc_parts[par][:, :], start=True, stop=True).then_inc(ready, 1)

                def spread_c(n):
                    if drains(k) and (cs > NC - 2 or n >= 2):
                        pe.wait_ge(c_copied, DS * (cs - (NC - 2)) + (n - 1))
                        spread(c_bank, None, c_ready, DS + n, n)
                    else:
                        spread(c_bank, hc_done, c_ready, DS + n, n)

                def mid_slot(s):
                    shared_steps(s, 0.5)
                    if scan and s > 0:
                        spread_c(s)

                def state_sum(n, c):
                    if n == 0:
                        pe.wait_ge(mixed_copied, NC)
                        pe.wait_ge(ident_ready, 2)
                        pe.wait_ge(y_skip, k - 2)
                    pe.wait_ge(hc_done, DS * c + n + 1)
                    for h in range(HV):
                        last = nc.tensor.matmul(y_bank[h][:, :], ident, hc[n % 2][:, h, :], start=(n == 0),
                                                stop=(n == DS - 1))
                    last.then_inc(y_summed, 1)

                def shared_steps(s, part):
                    for name, slot, stage in SHARED:
                        now = planned(k, s, stage)
                        if now is not None and slot == now + part and (pre if stage == "pre" else post):
                            shared_step(name)

                for s in range(16):
                    if scan and s == 0:
                        pe.wait_ge(low_ready, cs + 1)
                        pe.wait_ge(mid_ready, cs + 1)
                        spread(b_bank, dbu_done, b_ready, 0, 0)
                    if scan and s < DS - 1:
                        spread(b_bank, dbu_done, b_ready, s + 1, s + 1)
                    if scan and s == 0:
                        spread_c(0)
                    shared_steps(s, 0)
                    if adj:
                        if s == 0:
                            wait(pe, mixed_copied, k)
                        r = s % RING
                        if not scan:
                            if isinstance(k, int) and k == 0 and s * PB % GB == 0:
                                pe.wait_ge(xn_ready, s * PB // GB + 1)
                        pe.wait_ge(adj_in[r], 16 * (PIECES // RING) * k + 16 * (s // RING + 1))
                        for b in range(PB):
                            if b == PB // 2:
                                mid_slot(s)
                            j = s * PB + b
                            a = ring[:, (r * PB + b) * CH:(r * PB + b + 1) * CH]
                            last = nc.tensor.matmul(mixed[:, :], xn[:, j, :], a, start=(j == 0), stop=(j == BLK - 1))
                        last.then_inc(adj_used, 1)
                    else:
                        mid_slot(s)
                        if s < 2 and drains(k - 1):
                            state_sum(DS - 2 + s, cs - 1)
                        if scan and s >= 2:
                            state_sum(s - 2, cs)

            iterations(pe, step)

            pe.wait_ge(bias_ready, 1)
            pe.wait_ge(lstm_init, 2)
            pe.wait_ge(xls_in, 16)
            pass_no = pe.alloc_register("pe_pass")
            go_on = pe.alloc_register("pe_go")
            pe.reg_mov(pass_no, 0)
            pe.reg_mov(go_on, 1)

            def input_part(t, tau_par, b, alone=False):
                g = gates[b][tau_par]
                nc.tensor.matmul(g[:, 0:BG * HS], bias_w[:, :], bias_cols, start=True, stop=False, skip_group_check=True)
                for q in range(4):
                    last = nc.tensor.matmul(g[:, q * HS:(q + 1) * HS], W("w_ih", q * D, (q + 1) * D),
                                     xls[:, b * (NC // 2):(b + 1) * (NC // 2), bass.ds(t * SPC, SPC)],
                                     start=False, stop=alone and q == 3, skip_group_check=True)
                if alone:
                    last.then_inc(gates_ready, 1)

            def hidden_part(t, tau_par, b, done):
                g = gates[b][tau_par]
                wait(pe, hid_ready, done)
                for q in range(4):
                    last = nc.tensor.matmul(g[:, q * HS:(q + 1) * HS], W("w_hh", q * D, (q + 1) * D),
                                            hs[:, t, b * HS:(b + 1) * HS],
                                            start=False, stop=(q == 3), skip_group_check=True)
                last.then_inc(gates_ready, 1)

            def two_steps(t, done, first, last_pair, from_zero=False):
                for e in range(2):
                    for b in range(2):
                        if not (from_zero and e == 0):
                            hidden_part(t + e, e, b, 0 if first and e == 0 else done + 2 * (t + e) + (b - 1))
                        if not (last_pair and e == 1):
                            input_part(t + e + 1, 1 - e, b)

            def run_steps(begin, done, from_zero=False):
                for b in range(2):
                    if from_zero and b == 1:
                        pe.wait_ge(xl_ready, NC)
                    input_part(begin, 0, b, from_zero)
                two_steps(begin, done, True, False, from_zero)
                with pe.Fori(begin + 2, SEG - 3, 2) as t:
                    two_steps(t, done, False, False)
                two_steps(SEG - 2, done, False, True)

            run_steps(SEG - WARM, -2 * (SEG - WARM), from_zero=True)
            pe.wait_ge(guess_ready, 1)
            with pe.While(lambda: pe.snap(go_on)):
                pn = pe.snap(pass_no)
                run_steps(0, 2 * SEG * pn + 2 * WARM)
                pe.wait_ge(agree_ready, pn + 1)
                nc.tensor.matmul(count_ps[:, 0:1], ones_w[:, :], agree, start=True, stop=True).then_inc(agree_sum, 1)
                pe.wait_ge(flag_ready, pn + 1)
                pe.sem_inc(flag_seen, 1)
                pe.reg_load(go_on, flag[0:1, 0:1])
                pe.reg_add(pass_no, pass_no, 1)

            pe.wait_ge(lstm_init, 3)

            def chunk(i, q):
                wait(pe, wsel_ready, i - 1)
                nc.tensor.matmul(l_bank[q][:, :], wlin, hs[:, 1:SEG + 1, bass.ds(i * SPC, SPC)],
                                 start=True, stop=True).then_inc(logit_ready, 1)

            by_chunk(pe, chunk)

        @block.scalar
        def _(act):
            act.dma_start(bias_in[0:4, :], lstm_bias).then_inc(bias_loaded, 16)
            act.dma_start(bias_in[32:36, :], lstm_bias).then_inc(bias_loaded, 16)
            act.dma_start(bias_in[64:68, :], lstm_bias).then_inc(bias_loaded, 16)
            act.preload_act_table_set(LN_EXP)
            act.wait_ge(consts_ready, 1)
            for g in range(XG):
                blk = slice(GB * g, GB * g + GB)
                act.wait_ge(row_centred, g + 1)
                if g:
                    act.wait_ge(row_var, g)
                nc.scalar.activation(sq_rows, xn[:, blk, :], ACT.Square).then_inc(row_sq, 1)
                act.wait_ge(row_var, g + 1)
                nc.scalar.activation(stat[:, 2, blk], stat[:, 1, blk], ACT.Ln,
                                     bias=eps[:, :], scale=1.0 / D).then_inc(row_ln, 1)
                act.wait_ge(row_ln, g + 1)
                nc.scalar.activation(stat[:, 3, blk], stat[:, 2, blk], ACT.Exp,
                                     scale=-0.5).then_inc(row_rstd, 1)
            act.wait_ge(consts_in, 32)
            o = VOFF["a_log"]
            nc.scalar.activation(a_neg[:, :], v_sb[:, o:o + HV * DS], ACT.Exp).then_inc(init_done, 1)

            def step(k, par, adj, pre, scan, post):
                cs, q = k - 2, 1 - par

                def written(name):
                    act.wait_ge(shared_written, shared_index(name, k, pre, post) + 1)

                def pre_part(s):
                    if s == 0:
                        written("gcn")
                        nc.scalar.activation(ht, shared[:, :], ACT.Relu, bias=V("gcn_b")).then_inc(shared_read, 1)
                    if s == 1:
                        act.wait_ge(shared_read, shared_index("mean", k, pre, post) + 1)
                        nc.scalar.activation(sq, ht, ACT.Square).then_inc(squared, 1)
                    if s == 2:
                        written("var")
                        nc.scalar.activation(rs, shared[:, :], ACT.Ln, bias=eps[:, :]).then_inc(shared_read, 1)
                        act.wait_ge(shared_read, shared_index("var", k, pre, post) + 1)
                        nc.scalar.activation(rs, rs, ACT.Exp, scale=-0.5).then_inc(rstd_ready, 1)
                    if s == 3:
                        act.wait_ge(hn_ready, k)
                        nc.scalar.activation(ht, ht, ACT.Identity, bias=V("ln_b"), scale=V("ln_g")).then_inc(h_ready, 1)
                    if s == 5:
                        for h in range(HV):
                            written(f"xc{h}")
                            nc.scalar.activation(xc[q][:, h, HALO:HALO + CH], shared[:, :], ACT.Copy).then_inc(shared_read, 1)
                        act.wait_ge(shared_read, shared_index("xc1", k, pre, post) + 1)
                        act.wait_ge(halo_ready, k)
                        for h in range(HV):
                            last = nc.scalar.activation(wd[:, h, :], xc[q][:, h, 0:CH], ACT.Identity,
                                                        bias=V("conv_b", h), scale=V("conv_w", h * TAPS))
                        last.then_inc(tap_ready, 1)
                        nc.scalar.activation(xc[1 - q][:, :, 0:HALO], xc[q][:, :, CH:CH + HALO], ACT.Copy).then_inc(halo_ready, 1)
                    if s == 6:
                        for h in range(HV):
                            written(f"z{h}")
                            nc.scalar.activation(sz[q][:, h, :], shared[:, :], ACT.Copy).then_inc(shared_read, 1)
                    if s == 8:
                        act.wait_ge(tap_done, HALO * k)
                        nc.scalar.activation(u[q], wd, ACT.Silu).then_inc(u_ready, 1)
                        act.wait_ge(shared_read, shared_index("z1", k, pre, post) + 1)
                        nc.scalar.activation(sz[q], sz[q], ACT.Silu).then_inc(sz_ready, 1)
                        act.preload_act_table_set(LN_EXP)
                    if s == 9:
                        written("dbc")
                        nc.scalar.activation(dbc[0:XPW, :], shared[0:XPW, :], ACT.Copy).then_inc(shared_read, 1)
                        act.wait_ge(shared_read, shared_index("dbc", k, pre, post) + 1)
                        nc.scalar.activation(bc_parts[q][:, :], dbc[0:PARTS * BC, :], ACT.Copy).then_inc(high_ready, 1)
                    if s == 10:
                        for h in range(HV):
                            written(f"dt{h}")
                            nc.scalar.activation(wa[:, h, :], shared[:, :], ACT.Relu, bias=V("b_dt", h)).then_inc(pos_dt, 1)
                            nc.scalar.activation(wb[:, h, :], shared[:, :], ACT.Abs, bias=V("b_dt", h)).then_inc(shared_read, 1)
                    if s == 11:
                        act.wait_ge(shared_read, shared_index("dt1", k, pre, post) + 1)
                        nc.scalar.activation(wb, wb, ACT.Exp, scale=-1.0).then_inc(exp_dt, 1)
                        act.wait_ge(exp_dt, k)
                        nc.scalar.activation(wc, wb, ACT.Identity, bias=1.0).then_inc(one_dt, 1)
                        act.wait_ge(one_dt, k)
                        nc.scalar.activation(wd, wc, ACT.Ln).then_inc(log_dt, 1)
                    if s == 12:
                        act.wait_ge(r1_ready, k)
                        nc.scalar.activation(bc_mid[:, :], r1[0:PARTS * BC, :], ACT.Copy).then_inc(mid_rounded, 1)
                        act.wait_ge(mid_rounded, k)
                        nc.scalar.activation(bc_parts[q][BC:2 * BC, :], bc_mid[BC:2 * BC, :], ACT.Copy).then_inc(mid_ready, 1)

                def post_part(s):
                    if s == 0:
                        for h in range(HV):
                            last = nc.scalar.activation(yv[:, h, :], u[q][:, h, :], ACT.Copy, scale=V("d_skip", h))
                        last.then_inc(skip_ready, 1)
                    if s == 4:
                        act.wait_ge(shared_read, shared_index("out", k, pre, post) + 1)
                        act.dma_start(x1_dram[k - 3], x1c).then_inc(x1_stored, 16)
                    if s == 5:
                        act.wait_ge(shared_read, shared_index("pmean", k, pre, post) + 1)
                        nc.scalar.activation(psq, xd, ACT.Square).then_inc(psq_ready, 1)
                    if s == 7:
                        written("pvar")
                        nc.scalar.activation(prs, shared[:, :], ACT.Ln, bias=eps[:, :]).then_inc(shared_read, 1)
                        act.wait_ge(shared_read, shared_index("pvar", k, pre, post) + 1)
                        nc.scalar.activation(prs, prs, ACT.Exp, scale=-0.5).then_inc(prstd_ready, 1)
                    if s == 12:
                        if not (isinstance(k, int) and k - 3 >= DIRECT):
                            act.wait_ge(xl_ready, k - 2)
                            act.dma_start(xl_dram[k - 3], xlc).then_inc(xl_stored, 16)

                def copy_c(n):
                    act.wait_ge(c_ready, DS * cs + n + 1)
                    act.wait_ge(adj_used, PIECES * NC)
                    act.wait_ge(hc_done, DS * cs + (n - 1))
                    nc.scalar.activation(c_sb[n % 2], c_bank[n % 2][:, :], ACT.Copy).then_inc(c_copied, 1)

                for s in range(16):
                    if scan and drains(k) and s >= 1:
                        copy_c(s - 1)
                    if pre and s == 0:
                        act.wait_ge(adj_used, PIECES * k)
                        nc.scalar.activation(m1, mixed[:, :], ACT.Copy).then_inc(mixed_copied, 1)
                    if scan:
                        if s == 0:
                            act.wait_ge(dt_ready, cs + 1)
                        for h in range(HV):
                            if drains(k):
                                act.wait_ge(scan_done, HV * DS * cs + (HV * (s - 2) + h + 1))
                            else:
                                wait(act, scan_done, HV * DS * cs + (HV * (s - 1) + h + 1))
                            nc.scalar.activation(da_drain[s % 2][h] if drains(k) else da[h], dt[par][:, h, :], ACT.Exp,
                                                 scale=a_neg[:, h * DS + s:h * DS + s + 1]).then_inc(da_ready, 1)
                    if pre:
                        pre_part(planned(k, s, "pre"))
                    if post:
                        post_part(planned(k, s, "post"))
                if scan and drains(k):
                    copy_c(DS - 1)

            iterations(act, step)

            act.preload_act_table_set("sigmoid_and_others")
            act.wait_ge(lstm_init, 2)
            act.wait_ge(bias_ready, 2)
            pass_no = act.alloc_register("act_pass")
            go_on = act.alloc_register("act_go")
            act.reg_mov(pass_no, 0)
            act.reg_mov(go_on, 1)
            def run_steps(begin, base):
                with act.Fori(begin, SEG - 1, 2) as t:
                    for e in range(2):
                        for b in range(2):
                            done = base + 2 * t + (2 * e + b + 1)
                            g = gates[b][e]
                            act.wait_ge(gates_ready, done)
                            nc.scalar.activation(tg_c_half[:, b, 0, :], g[:, 2 * HS:3 * HS], ACT.Tanh, bias=go_bias[:, 0:1])
                            nc.scalar.activation(sg[b][:, 0:2 * HS], g[:, 0:2 * HS], ACT.Sigmoid).then_inc(sg_ready, 1)
                            nc.scalar.activation(sg[b][:, 2 * HS:3 * HS], g[:, 3 * HS:4 * HS], ACT.Sigmoid,
                                                 bias=go_bias[:, 1:2])
                            act.wait_ge(cell_ready, done)
                            nc.scalar.activation(tc[b], c_st[:, b * HS:(b + 1) * HS], ACT.Tanh).then_inc(tc_ready, 1)

            run_steps(SEG - WARM, -2 * (SEG - WARM))
            with act.While(lambda: act.snap(go_on)):
                pn = act.snap(pass_no)
                run_steps(0, 2 * SEG * pn + 2 * WARM)
                act.wait_ge(flag_ready, pn + 1)
                act.sem_inc(flag_seen, 1)
                act.reg_load(go_on, flag[0:1, 0:1])
                act.reg_add(pass_no, pass_no, 1)

            def scaled_sum(i, q):
                act.wait_ge(inc_ready, i + 1)
                wait(act, bwd_done, i - 1)
                nc.scalar.activation(inc_bw[q], inc[q][:, 1:CH + 1], ACT.Copy, scale=negbw[:, :]).then_inc(inc_bw_ready, 1)

            def chunk(i, q):
                wait(act, fwd_done, i - 1)
                nc.scalar.activation(h2[q].rearrange("p (s t) -> p t s", s=SPC),
                                     hs[:, 1:SEG + 1, bass.ds(i * SPC, SPC)], ACT.Copy, scale=2.0).then_inc(h2_ready, 1)
                if not (isinstance(i, int) and i == 0):
                    scaled_sum(i - 1, 1 - q)

            act.wait_ge(lstm_init, 3)
            by_chunk(act, chunk)
            scaled_sum(NC - 1, 1)

        @block.gpsimd
        def _(pool):
            nc.gpsimd.memset(sel[:, :], 0.0).then_inc(sel_ready, 1)
            view = sel[:, :].rearrange("p (n m) -> p n m", m=P)
            for g in range(PARTS):
                pool.wait_ge(sel_ready, g + 1)
                nc.gpsimd.affine_select(out=view, in_=view, compare_op=ALU.not_equal, fill=1.0, base=-BC * g,
                                        pattern=[[-1, BC], [0, P]], channel_multiplier=1).then_inc(sel_ready, 1)
            pool.wait_ge(consts_in, 32)

            def step(k, par, adj, pre, scan, post):
                cs, q = k - 2, 1 - par

                def pre_part(s):
                    if drains(k):
                        return
                    if s == 12:
                        pool.wait_ge(log_dt, k)
                        pool.wait_ge(rem_dt, k)
                        nc.gpsimd.tensor_tensor(out=wb, in0=wd, in1=wb, op=ALU.subtract).then_inc(sum_dt, 1)
                    if s == 13:
                        pool.wait_ge(sum_dt, k)
                        pool.wait_ge(pos_dt, HV * k)
                        nc.gpsimd.tensor_tensor(out=dt[q], in0=wa, in1=wb, op=ALU.add).then_inc(dt_ready, 1)
                    if s == 14:
                        pool.wait_ge(dt_ready, k)
                        nc.gpsimd.tensor_tensor(out=dtu[q], in0=dt[q], in1=u[q], op=ALU.mult).then_inc(dtu_ready, 1)

                def post_part(s):
                    if s == 0 and not drains(k):
                        pool.wait_ge(y_added, (DS - 1) * (k - 2))
                        pool.wait_ge(skip_ready, k - 2)
                        nc.gpsimd.tensor_tensor(out=yv, in0=yv, in1=acc, op=ALU.add).then_inc(y_skip, 1)
                        pool.wait_ge(y_skip, k - 2)
                        pool.wait_ge(sz_ready, k - 2)
                        nc.gpsimd.tensor_tensor(out=yv, in0=yv, in1=sz[q], op=ALU.mult).then_inc(y_ready, 1)
                    if s == 8 and not (isinstance(k, int) and k == NC + 2):
                        make_xl(pool, nc.gpsimd, k)

                def add(n):
                    pool.wait_ge(hc_done, DS * cs + n + 1)
                    if n > 1:
                        pool.wait_ge(y_added, (DS - 1) * cs + (n - 1))
                    nc.gpsimd.tensor_tensor(out=acc, in0=hc[0] if n == 1 else acc, in1=hc[n % 2],
                                            op=ALU.add).then_inc(y_added, 1)

                def make_hc(n):
                    pool.wait_ge(c_copied, DS * (cs - (NC - 2)) + n + 1)
                    pool.wait_ge(scan_done, HV * DS * cs + HV * (n + 1))
                    if n < 2:
                        pool.wait_ge(y_added, (DS - 1) * (NC - 2))
                    wait(pool, y_summed, DS * (cs - (NC - 2)) + (n - 1))
                    nc.gpsimd.tensor_tensor(out=hc[n % 2], in0=hb[n % 2],
                                            in1=c_sb[n % 2].unsqueeze(1).broadcast_to([P, HV, CH]),
                                            op=ALU.mult).then_inc(hc_done, 1)

                if drains(k) and k == NC:
                    pool.wait_ge(adj_used, PIECES * NC)
                    nc.gpsimd.memset(ident, 0.0).then_inc(ident_ready, 1)
                    pool.wait_ge(ident_ready, 1)
                    nc.gpsimd.affine_select(out=ident, in_=ident, compare_op=ALU.not_equal, fill=1.0, base=0,
                                            pattern=[[-1, P]], channel_multiplier=1).then_inc(ident_ready, 1)
                for s in range(16):
                    if post and s == 0:
                        post_part(s)
                    if scan and drains(k):
                        make_hc(s)
                    elif scan and s >= 2:
                        add(s - 1)
                    if pre:
                        pre_part(s)
                    if post and s > 0:
                        post_part(planned(k, s, "post"))
                if scan and not drains(k):
                    add(DS - 1)

            iterations(pool, step)

            def chunk(i, q):
                o = fin_all[:, bass.ds(i * CH, CH)]
                pool.wait_ge(fwd_done, i + 1)
                pool.wait_ge(inc_bw_ready, i + 1)
                nc.gpsimd.tensor_tensor(out=o, in0=inc_bw[q], in1=o, op=ALU.add).then_inc(bwd_done, 1)

            by_chunk(pool, chunk)

        @block.vector
        def _(dve):
            nc.vector.memset(mean_w[:, :], 1.0 / D)
            nc.vector.memset(eps[:, :], EPS)
            nc.vector.memset(hstate[:, :], 0.0)
            nc.vector.memset(xc[0][:, :, 0:HALO], 0.0).then_inc(halo_ready, 1)
            nc.vector.memset(ones_w[:, :], 1.0).then_inc(consts_ready, 1)
            def blocks(g):
                return slice(GB * g, GB * g + GB)

            def spread(k, g):
                return stat[:, k, blocks(g)].unsqueeze(2).broadcast_to([P, GB, D])

            def centre(g):
                dve.wait_ge(x_in[g], 16)
                nc.vector.reduce_sum(stat[:, 0, blocks(g)], xn[:, blocks(g), :], axis=AX.X).then_inc(row_sum, 1)
                dve.wait_ge(row_sum, g + 1)
                nc.vector.tensor_scalar(stat[:, 0, blocks(g)], stat[:, 0, blocks(g)], 1.0 / D, None, ALU.mult).then_inc(row_mean, 1)
                dve.wait_ge(row_mean, g + 1)
                nc.vector.tensor_tensor(out=xn[:, blocks(g), :], in0=xn[:, blocks(g), :], in1=spread(0, g),
                                        op=ALU.subtract).then_inc(row_centred, 1)

            centre(0)
            for g in range(XG):
                dve.wait_ge(row_sq, g + 1)
                nc.vector.reduce_sum(stat[:, 1, blocks(g)], sq_rows, axis=AX.X).then_inc(row_var, 1)
                if 0 < g < XG - 1:
                    centre(g + 1)
                dve.wait_ge(row_rstd, g + 1)
                nc.vector.tensor_tensor(out=xn[:, blocks(g), :], in0=xn[:, blocks(g), :], in1=spread(3, g),
                                        op=ALU.mult).then_inc(xn_ready, 1)
                if g == 0:
                    centre(1)
            dve.wait_ge(init_done, 1)
            nc.vector.tensor_scalar(a_neg[:, :], a_neg[:, :], -1.0, None, ALU.mult).then_inc(init_done, 1)
            nc.vector.tensor_scalar(negbw[:, :], V("bw"), -1.0, None, ALU.mult)
            nc.vector.memset(bias_w[:, :], 0.0).then_inc(bias_ready, 1)
            dve.wait_ge(bias_loaded, 48)
            n = [0]

            def link(ins):
                n[0] += 1
                ins.then_inc(check_step, 1)
                dve.wait_ge(check_step, n[0])

            for i in range(2):
                nc.vector.tensor_tensor(out=go_bias[:, i:i + 1], in0=V("go_ih", i), in1=V("go_hh", i), op=ALU.add)
            full, tail = bias_in[:, 0:P], bias_in[:, P:2 * P]
            for i in range(PARTS):
                r = slice(32 * i, 32 * i + 4)
                link(nc.vector.tensor_tensor(out=full[r], in0=full[r], in1=tail[r], op=ALU.add))
                link(nc.vector.tensor_copy(bias_mid[r, :], full[r]))
                for _ in range(i):
                    link(nc.vector.tensor_tensor(out=full[r], in0=full[r], in1=bias_mid[r, :], op=ALU.subtract))
                    link(nc.vector.tensor_copy(bias_mid[r, :], full[r]))
                if i == 0:
                    dve.wait_ge(bias_ready, 1)
                link(nc.vector.tensor_copy(bias_w[r, :], bias_mid[r, :]))
            dve.sem_inc(bias_ready, 1)

            def step(k, par, adj, pre, scan, post):
                cs, q = k - 2, 1 - par

                def written(name):
                    dve.wait_ge(shared_written, shared_index(name, k, pre, post) + 1)

                def side_part(slot):
                    s, t = planned(k, slot, "pre"), planned(k, slot, "post")
                    if drains(k):
                        if post and slot == (1 if k == NC else 2):
                            finish_y()
                        if pre and s in (12, 13, 14):
                            make_dt(s)
                    if pre and s == 1:
                        written("mean")
                        nc.vector.tensor_tensor(out=ht, in0=ht, in1=shared[:, :], op=ALU.subtract).then_inc(shared_read, 1)
                    if post and t == 3:
                        written("out")
                        dve.wait_ge(xt_in[q], 8 * (k - 3 - q) + 16)
                        wait(dve, x1_stored, 16 * (k - 3))
                        nc.vector.tensor_tensor(out=x1c, in0=xt[q], in1=shared[:, :], op=ALU.add).then_inc(shared_read, 1)
                    if pre and s == 3:
                        dve.wait_ge(rstd_ready, k)
                        nc.vector.tensor_tensor(out=ht, in0=ht, in1=rs, op=ALU.mult).then_inc(hn_ready, 1)
                    if post and t == 4:
                        written("pmean")
                        nc.vector.tensor_tensor(out=xd, in0=x1c, in1=shared[:, :], op=ALU.subtract).then_inc(shared_read, 1)
                    if pre and s in (6, 7):
                        for i in ((1,) if s == 6 else (2, 3)):
                            if i == 1:
                                dve.wait_ge(tap_ready, k)
                            else:
                                dve.wait_ge(tap_done, HALO * (k - 1) + (i - 1))
                            for h in range(HV):
                                last = nc.vector.scalar_tensor_tensor(
                                    out=wd[:, h, :], in0=xc[q][:, h, i:i + CH], scalar=V("conv_w", h * TAPS + i),
                                    in1=wd[:, h, :], op0=ALU.mult, op1=ALU.add)
                            last.then_inc(tap_done, 1)
                    if pre and s == 10:
                        dve.wait_ge(high_ready, k)
                        nc.vector.tensor_tensor(out=r1[0:PARTS * BC, :], in0=dbc[0:PARTS * BC, :], in1=bc_parts[q][:, :],
                                                op=ALU.subtract).then_inc(r1_ready, 1)
                    if pre and s == 12 and not drains(k):
                        dve.wait_ge(one_dt, k)
                        nc.vector.scalar_tensor_tensor(out=wb, in0=wc, scalar=-1.0, in1=wb, op0=ALU.add,
                                                       op1=ALU.subtract).then_inc(rem_dt, 1)
                    if pre and s == 13:
                        dve.wait_ge(mid_rounded, k)
                        nc.vector.tensor_tensor(out=bc_parts[q][2 * BC:3 * BC, :], in0=r1[2 * BC:3 * BC, :],
                                                in1=bc_mid[2 * BC:3 * BC, :], op=ALU.subtract).then_inc(low_ready, 1)

                def finish_y():
                    dve.wait_ge(skip_ready, k - 2)
                    if k == NC:
                        dve.wait_ge(y_added, (DS - 1) * (NC - 2))
                        nc.vector.tensor_tensor(out=yv, in0=yv, in1=acc, op=ALU.add).then_inc(y_skip, 1)
                    else:
                        dve.wait_ge(y_summed, DS * (k - NC))
                        for h in range(HV):
                            last = nc.vector.tensor_tensor(out=yv[:, h, :], in0=yv[:, h, :], in1=y_bank[h][:, :], op=ALU.add)
                        last.then_inc(y_skip, 1)
                    dve.wait_ge(y_skip, k - 2)
                    dve.wait_ge(sz_ready, k - 2)
                    nc.vector.tensor_tensor(out=yv, in0=yv, in1=sz[q], op=ALU.mult).then_inc(y_ready, 1)

                def make_dt(s):
                    if s == 12:
                        dve.wait_ge(log_dt, k)
                        nc.vector.scalar_tensor_tensor(out=wb, in0=wc, scalar=-1.0, in1=wb, op0=ALU.add,
                                                       op1=ALU.subtract).then_inc(rem_dt, 1)
                        dve.wait_ge(rem_dt, k)
                        nc.vector.tensor_tensor(out=wb, in0=wd, in1=wb, op=ALU.subtract).then_inc(sum_dt, 1)
                    if s == 13:
                        dve.wait_ge(sum_dt, k)
                        dve.wait_ge(pos_dt, HV * k)
                        nc.vector.tensor_tensor(out=dt[q], in0=wa, in1=wb, op=ALU.add).then_inc(dt_ready, 1)
                    if s == 14:
                        dve.wait_ge(dt_ready, k)
                        nc.vector.tensor_tensor(out=dtu[q], in0=dt[q], in1=u[q], op=ALU.mult).then_inc(dtu_ready, 1)

                def both(ap):
                    return ap[:, :].unsqueeze(1).broadcast_to([P, HV, CH])

                def make_dbu(n):
                    dve.wait_ge(b_ready, DS * cs + n + 1)
                    wait(dve, scan_done, HV * (DS * cs + n - 1) if isinstance(cs, int) else HV * DS * cs + HV * (n - 1))
                    nc.vector.tensor_tensor(out=dbu[n % 2], in0=dtu[par], in1=both(b_bank[n % 2]),
                                            op=ALU.mult).then_inc(dbu_done, 1)

                def make_hc(n):
                    dve.wait_ge(c_ready, DS * cs + n + 1)
                    dve.wait_ge(scan_done, HV * DS * cs + HV * (n + 1))
                    wait(dve, y_added, (DS - 1) * cs + (max(n - 2, 1) if n >= 2 else n - 1))
                    nc.vector.tensor_tensor(out=hc[n % 2], in0=hb[n % 2], in1=both(c_bank[n % 2]),
                                            op=ALU.mult).then_inc(hc_done, 1)
                    save_state(n)

                def save_state(n):
                    nc.vector.tensor_copy(hstate[:, HV * n:HV * n + HV], hb[n % 2][:, :, CH - 1]).then_inc(state_saved, 1)

                def after_scan(n):
                    if drains(k):
                        dve.wait_ge(scan_done, HV * DS * cs + HV * (n + 1))
                        save_state(n)
                    else:
                        make_hc(n)

                def lstm_setup():
                    dve.wait_ge(adj_used, PIECES * NC)
                    dve.wait_ge(dtu_ready, NC)
                    nc.vector.memset(hs[:, 0, :], 0.0)
                    if WARM < SEG:
                        nc.vector.memset(hs[:, SEG - WARM, :], 0.0)
                    nc.vector.memset(c_in, 0.0)
                    nc.vector.memset(passes, 0.0)
                    nc.vector.tensor_tensor(out=tie, in0=V("b_lin", 0), in1=V("b_lin", 1), op=ALU.subtract)
                    nc.vector.memset(c_st, 0.0).then_inc(lstm_init, 1)
                    dve.wait_ge(lstm_init, 1)
                    nc.vector.tensor_tensor(out=wlin, in0=V("w_lin", 1).broadcast_to([P, P]),
                                            in1=V("w_lin", 0).broadcast_to([P, P]), op=ALU.subtract).then_inc(lstm_init, 1)

                if isinstance(k, int) and k == NC + 2:
                    lstm_setup()
                for s in range(16):
                    side_part(s)
                    if not scan:
                        continue
                    if s == 0:
                        dve.wait_ge(dtu_ready, cs + 1)
                        make_dbu(0)
                    if s < DS - 1:
                        make_dbu(s + 1)
                    for h in range(HV):
                        dve.wait_ge(da_ready, HV * DS * cs + (HV * s + h + 1))
                        if h == 0:
                            dve.wait_ge(dbu_done, DS * cs + s + 1)
                            wait(dve, state_saved, DS * cs + (s - 1))
                            wait(dve, hc_done, DS * cs + (s - 1))
                        nc.vector.tensor_tensor_scan(hb[s % 2][:, h, :], da_drain[s % 2][h] if drains(k) else da[h], dbu[s % 2][:, h, :],
                                                     hstate[:, HV * s + h:HV * s + h + 1],
                                                     ALU.mult, ALU.add).then_inc(scan_done, 1)
                    if s >= 1:
                        after_scan(s - 1)
                if scan:
                    after_scan(DS - 1)
                if isinstance(k, int) and k == NC + 2:
                    make_xl(dve, nc.vector, k)

            iterations(dve, step)

            pass_no = dve.alloc_register("dve_pass")
            go_on = dve.alloc_register("dve_go")
            dve.reg_mov(pass_no, 0)
            dve.reg_mov(go_on, 1)
            checks = 5

            def run_steps(begin, base):
                with dve.Fori(begin, SEG) as t:
                    for b in range(2):
                        seg = slice(b * HS, (b + 1) * HS)
                        done = base + 2 * t + (b + 1)
                        dve.wait_ge(sg_ready, done)
                        nc.vector.tensor_tensor(out=ig_fc[b].rearrange("p (k s) -> p k s", k=2),
                                                in0=sg[b][:, 0:2 * HS].rearrange("p (k s) -> p k s", k=2),
                                                in1=tg_c_half[:, b], op=ALU.mult).then_inc(ig_fc_ready, 1)
                        dve.wait_ge(ig_fc_ready, done)
                        nc.vector.tensor_tensor(out=c_st[:, seg], in0=ig_fc[b][:, 0:HS], in1=ig_fc[b][:, HS:2 * HS],
                                                op=ALU.add).then_inc(cell_ready, 1)
                        dve.wait_ge(tc_ready, done)
                        nc.vector.tensor_tensor(out=hs[:, t + 1, seg], in0=sg[b][:, 2 * HS:3 * HS], in1=tc[b],
                                                op=ALU.mult).then_inc(hid_ready, 1)

            run_steps(SEG - WARM, -2 * (SEG - WARM))
            dve.wait_ge(hid_ready, 2 * WARM)
            nc.vector.tensor_copy(hs[:, 0, 1:NSEG], hs[:, SEG, 0:NSEG - 1])
            link(nc.vector.tensor_copy(c_in[:, 1:NSEG], c_st[:, 0:NSEG - 1]))
            nc.vector.tensor_copy(c_st, c_in).then_inc(guess_ready, 1)
            dve.wait_ge(guess_ready, 1)
            links_before = n[0]
            with dve.While(lambda: dve.snap(go_on)):
                pn = dve.snap(pass_no)
                run_steps(0, 2 * SEG * pn + 2 * WARM)
                base = checks * pn + links_before
                k = [0]

                def then(ins):
                    k[0] += 1
                    ins.then_inc(check_step, 1)
                    dve.wait_ge(check_step, base + k[0])

                dve.wait_ge(hid_ready, 2 * SEG * pn + 2 * (WARM + SEG))
                E = NSEG - 1
                nc.vector.tensor_tensor(out=diff[:, 0:E], in0=hs[:, SEG, 0:E], in1=hs[:, 0, 1:NSEG], op=ALU.subtract)
                nc.vector.tensor_scalar(passes, passes, 1.0, None, ALU.add)
                nc.vector.tensor_tensor(out=c_tol, in0=c_in[:, 1:NSEG], in1=c_in[:, 1:NSEG], op=ALU.mult)
                then(nc.vector.tensor_tensor(out=diff[:, E:2 * E], in0=c_st[:, 0:E], in1=c_in[:, 1:NSEG], op=ALU.subtract))
                nc.vector.tensor_copy(hs[:, 0, 1:NSEG], hs[:, SEG, 0:E])
                nc.vector.tensor_copy(c_in[:, 1:NSEG], c_st[:, 0:E])
                nc.vector.tensor_scalar(c_tol, c_tol, 1.0, TOL * TOL, ALU.max, ALU.mult)
                then(nc.vector.tensor_tensor(out=diff, in0=diff, in1=diff, op=ALU.mult))
                nc.vector.tensor_scalar(diff[:, 0:E], diff[:, 0:E], TOL * TOL, None, ALU.is_le)
                then(nc.vector.tensor_tensor(out=diff[:, E:2 * E], in0=diff[:, E:2 * E], in1=c_tol, op=ALU.is_le))
                then(nc.vector.tensor_scalar(alive, passes, float(NSEG), None, ALU.is_lt))
                nc.vector.reduce_sum(agree, diff, axis=AX.X).then_inc(agree_ready, 1)
                then(nc.vector.tensor_copy(c_st, c_in))
                dve.wait_ge(agree_sum, pn + 1)
                nc.vector.scalar_tensor_tensor(out=flag[:, :], in0=count_ps[0:1, 0:1], scalar=float(2 * E * P),
                                               in1=alive[0:1, :], op0=ALU.is_lt, op1=ALU.mult).then_inc(flag_ready, 1)
                dve.wait_ge(flag_ready, pn + 1)
                dve.sem_inc(flag_seen, 1)
                dve.reg_load(go_on, flag[0:1, 0:1])
                assert k[0] == checks
                dve.reg_add(pass_no, pass_no, 1)
            dve.sem_inc(lstm_init, 1)

            nc.vector.memset(inc[1][:, CH:CH + 1], 0.0).then_inc(inc_set, 1)

            def chunk(i, q):
                dve.wait_ge(logit_ready, i + 1)
                wait(dve, inc_ready, i - 1)
                nc.vector.scalar_tensor_tensor(
                    out=wsel[q].rearrange("p (s t) -> p t s", s=SPC),
                    in0=l_bank[q][:, :].rearrange("p (t s) -> p t s", s=SPC), scalar=tie,
                    in1=hs[:, 1:SEG + 1, bass.ds(i * SPC, SPC)], op0=ALU.is_gt, op1=ALU.mult).then_inc(wsel_ready, 1)
                if isinstance(i, int) and i == 0:
                    dve.wait_ge(inc_set, 1)
                else:
                    dve.wait_ge(inc_ready, i)
                wait(dve, inc_bw_ready, i - 1)
                wait(dve, fwd_done, i - 1)
                nc.vector.tensor_copy(inc[q][:, 0:1], inc[1 - q][:, CH:CH + 1]).then_inc(carry_ready, 1)
                dve.wait_ge(wsel_ready, i + 1)
                nc.vector.tensor_tensor_scan(inc[q][:, 1:CH + 1], wsel[q], wsel[q], inc[1 - q][:, CH:CH + 1],
                                             ALU.add, ALU.bypass).then_inc(inc_ready, 1)
                if not (isinstance(i, int) and i == 0):
                    add_forward(i - 1, 1 - q)

            def add_forward(i, q):
                dve.wait_ge(h2_ready, i + 1)
                dve.wait_ge(carry_ready, i + 1)
                dve.wait_ge(inc_ready, i + 1)
                nc.vector.scalar_tensor_tensor(out=fin_all[:, bass.ds(i * CH, CH)], in0=inc[q][:, 0:CH], scalar=V("fw"),
                                               in1=h2[q], op0=ALU.mult, op1=ALU.add).then_inc(fwd_done, 1)

            by_chunk(dve, chunk)
            add_forward(NC - 1, 1)
            dve.wait_ge(inc_ready, NC)
            nc.vector.tensor_tensor(out=bw_total, in0=inc[1][:, CH:CH + 1], in1=V("bw"), op=ALU.mult).then_inc(total_ready, 1)
            dve.wait_ge(total_ready, 1)
            dve.wait_ge(x1_in, 16)
            for i in range(NC):
                o = fin_all[:, i * CH:(i + 1) * CH]
                dve.wait_ge(bwd_done, i + 1)
                nc.vector.scalar_tensor_tensor(out=o, in0=o, scalar=bw_total, in1=x1_all[:, i * CH:(i + 1) * CH],
                                               op0=ALU.add, op1=ALU.add).then_inc(out_ready, 1)


_INS = ["adj_t", "x_rows", "x_t", "weights", "vectors", "lstm_bias"]


def kernel(**inputs):
    import concourse.bacc as bacc
    from concourse.bass_utils import run_bass_kernel_spmd

    a = {k: np.asarray(v) for k, v in inputs.items()}
    g, f = "L0_gnn_", "L0_ffn_"
    x, adj = a["x"], a["adj"]

    def gate_rows(b):
        return b.reshape(4, D)

    def by_half(v):
        v = v.reshape(HV, P, -1)
        return np.concatenate([v[h] for h in range(HV)], axis=1)

    w_xp = a[g + "w_xp"]
    w_xp = np.concatenate([w_xp[:, DR:]] * PARTS + [w_xp[:, :DR]], axis=1)
    w_dt = np.zeros((P, DI), np.float32)
    w_dt[PARTS * BC:XPW] = a[g + "w_dt"]
    weights = np.concatenate([a[g + "gcn_w"], a[g + "w_in"], by_half(w_xp), w_dt, by_half(a[g + "w_out"]),
                              a[f + "W_ih"].T, a[f + "W_hh"].T], axis=1)

    def col(v):
        return v.reshape(P, 1)

    vectors = np.concatenate([col(a[g + "gcn_b"]), col(a[g + "ln_g"]), col(a[g + "ln_b"]), by_half(a[g + "conv_b"]),
                              by_half(a[g + "conv_w"]), by_half(a[g + "b_dt"]), by_half(a[g + "D_skip"]),
                              col(a[f + "fw_att"]), col(a[f + "bw_att"]), by_half(a[g + "A_log"]),
                              a[f + "W_lin"].T, np.broadcast_to(a[f + "b_lin"], (P, 2)),
                              gate_rows(a[f + "b_ih"])[2:].T, gate_rows(a[f + "b_hh"])[2:].T], axis=1)

    arrays = dict(
        adj_t=adj.reshape(NC, CH, P, BLK).transpose(0, 2, 3, 1).reshape(NC, P, BLK * CH),
        x_rows=x.reshape(P, BLK * D),
        x_t=x.reshape(NC, CH, D).transpose(0, 2, 1),
        weights=weights, vectors=vectors,
        lstm_bias=np.concatenate([gate_rows(a[f + "b_ih"]), gate_rows(a[f + "b_hh"])], axis=1),
    )
    arrays = {k: np.ascontiguousarray(v) for k, v in arrays.items()}
    nc = bacc.Bacc("TRN2", target_bir_lowering=False, num_devices=1)
    args = [nc.dram_tensor(n, arrays[n].shape, mybir.dt.from_np(arrays[n].dtype), kind="ExternalInput").ap() for n in _INS]
    out = nc.dram_tensor("out_t", (NC, P, CH), mybir.dt.float32, kind="ExternalOutput").ap()
    build(nc, *args, out)
    r = run_bass_kernel_spmd(nc, [arrays], core_ids=[0])
    return np.ascontiguousarray(r.results[0]["out_t"].transpose(0, 2, 1).reshape(N, D))
```
